# Optimizing a Trainium2 kernel written in Bass

```python
import numpy as np
import jax
import jax.numpy as jnp

def _softmax(x, axis=-1):
    return jax.nn.softmax(x, axis=axis)
def _gelu(x):
    return jax.nn.gelu(x, approximate=True)
def _silu(x):
    return jax.nn.silu(x)
def _sigmoid(x):
    return jax.nn.sigmoid(x)
def _layernorm(x, axis=-1, eps=1e-5):
    m = jnp.mean(x, axis=axis, keepdims=True)
    v = jnp.var(x, axis=axis, keepdims=True)
    return (x - m) / jnp.sqrt(v + eps)
def _scatter_add(tgt, idx, src, axis=0):
    return tgt.at[idx].add(src)
def _segment_sum(src, seg, n):
    return jax.ops.segment_sum(src, seg, n)

kernel_name = 'mk_conv_preact_d2_conv_nchw256_cc35da'

def setup_inputs(seed: int = 0):
    np.random.seed(seed)
    _w = jnp.asarray
    def _rec_inputs():
        import jax
        import jax.numpy as jnp
        _gk = jax.random.key(seed)
        x = 7.22e-05 + 1 * jax.random.normal(jax.random.fold_in(_gk, 1), (8, 256, 64, 64), jnp.float32)
        return x
    x = _rec_inputs()
    def _L0_conv_setup():
        import jax, jax.numpy as jnp
        import numpy as np
        from jax import lax
        DIM = 8
        HEADS = 32
        SCALE = 5
        EPS = 1e-15

        def _conv2d(x, w, groups=1, pad=0):
            return lax.conv_general_dilated(x, w, window_strides=(1, 1), padding=[(pad, pad), (pad, pad)], dimension_numbers=('NCHW', 'OIHW', 'NCHW'), feature_group_count=groups)
        key = jax.random.key(seed)
        ks = jax.random.split(key, 5)
        B, C, H, W = (8, 256, 64, 64)
        td = HEADS * DIM
        x = jax.random.normal(ks[0], (B, C, H, W), jnp.float32)
        w_qkv = jax.random.normal(ks[1], (3 * td, C, 1, 1), jnp.float32) * 0.05
        w_dw = jax.random.normal(ks[2], (3 * td, 1, SCALE, SCALE), jnp.float32) * 0.05
        w_pw = jax.random.normal(ks[3], (3 * td, 3 * td // (3 * HEADS), 1, 1), jnp.float32) * 0.1
        w_proj = jax.random.normal(ks[4], (C, td * 2, 1, 1), jnp.float32) * 0.05
        return {'x': x, 'w_qkv': w_qkv, 'w_dw': w_dw, 'w_pw': w_pw, 'w_proj': w_proj}
    _L0_conv_all = _L0_conv_setup()
    _L0_conv_in = {k: v for k, v in _L0_conv_all.items() if k in ('w_qkv', 'w_dw', 'w_pw', 'w_proj', )}
    del _L0_conv_all

    def _L1_conv_setup():
        import jax, jax.numpy as jnp
        import numpy as np
        B, C, H, W = (8, 256, 64, 64)
        NH, D = (4, 64)
        BLKQ = BLKK = 64
        TOPK_RATIO = 0.1
        EPS = 1e-06

        def _sla_forward(x, qkv_w, out_w, proj_lw, proj_lb):
            Bn, Cn, Hn, Wn = x.shape
            L = Hn * Wn
            nQ, nK = (L // BLKQ, L // BLKK)
            T = max(1, int(TOPK_RATIO * nK))
            xf = x.reshape(Bn, Cn, L)
            qkv = jnp.einsum('oc,bcl->bol', qkv_w, xf)
            q, k, v = jnp.split(qkv, 3, axis=1)

            def to_bhld(t):
                return t.reshape(Bn, NH, D, L).transpose(0, 1, 3, 2)
            q, k, v = (to_bhld(q), to_bhld(k), to_bhld(v))
            qr = q.reshape(Bn, NH, nQ, BLKQ, D)
            kr = k.reshape(Bn, NH, nK, BLKK, D)
            vr = v.reshape(Bn, NH, nK, BLKK, D)
            qb = qr.mean(axis=3)
            kb = kr.mean(axis=3)
            blk_scores = jnp.einsum('bhnd,bhmd->bhnm', qb, kb)
            _, lut = jax.lax.top_k(blk_scores, T)
            idx = lut[..., None, None]
            kg = jnp.take_along_axis(kr[:, :, None], idx, axis=3)
            vg = jnp.take_along_axis(vr[:, :, None], idx, axis=3)
            kg = kg.reshape(Bn, NH, nQ, T * BLKK, D)
            vg = vg.reshape(Bn, NH, nQ, T * BLKK, D)
            scale = D ** (-0.5)
            s = jnp.einsum('bhnqd,bhnkd->bhnqk', qr, kg) * scale
            p = jax.nn.softmax(s, axis=-1)
            o_s = jnp.einsum('bhnqk,bhnkd->bhnqd', p, vg)
            c_q = jax.nn.softmax(q, axis=-1)
            c_k = jax.nn.softmax(k, axis=-1)
            c_kr = c_k.reshape(Bn, NH, nK, BLKK, D)
            kvb = jnp.einsum('bhmkd,bhmke->bhmde', c_kr, vr)
            ksum = c_kr.sum(axis=3)
            sel = jax.nn.one_hot(lut, nK, dtype=q.dtype).sum(axis=3)
            comp = 1.0 - sel
            kv_q = jnp.einsum('bhnm,bhmde->bhnde', comp, kvb)
            ks_q = jnp.einsum('bhnm,bhmd->bhnd', comp, ksum)
            c_qr = c_q.reshape(Bn, NH, nQ, BLKQ, D)
            num = jnp.einsum('bhnqd,bhnde->bhnqe', c_qr, kv_q)
            den = jnp.einsum('bhnqd,bhnd->bhnq', c_qr, ks_q)
            o_l = num / (den[..., None] + EPS)
            o_l = jnp.einsum('bhnqd,ed->bhnqe', o_l, proj_lw) + proj_lb
            o = (o_s + o_l).reshape(Bn, NH, L, D)
            o = o.transpose(0, 1, 3, 2).reshape(Bn, Cn, L)
            o = jnp.einsum('oc,bcl->bol', out_w, o)
            return o.reshape(Bn, Cn, Hn, Wn)
        key = jax.random.key(seed)
        k1, k2, k3, k4, k5 = jax.random.split(key, 5)
        x = jax.random.normal(k1, (B, C, H, W), dtype=jnp.float32)
        qkv_w = jax.random.normal(k2, (3 * C, C), dtype=jnp.float32) / np.sqrt(C)
        out_w = jax.random.normal(k3, (C, C), dtype=jnp.float32) / np.sqrt(C)
        proj_lw = jax.random.normal(k4, (D, D), dtype=jnp.float32) * 0.02
        proj_lb = jax.random.normal(k5, (D,), dtype=jnp.float32) * 0.02
        return {'x': x, 'qkv_w': qkv_w, 'out_w': out_w, 'proj_lw': proj_lw, 'proj_lb': proj_lb}
    _L1_conv_all = _L1_conv_setup()
    _L1_conv_in = {k: v for k, v in _L1_conv_all.items() if k in ('qkv_w', 'out_w', 'proj_lw', 'proj_lb', )}
    del _L1_conv_all

    return {
        "x": x,
        "L0_conv_w_qkv": _L0_conv_in["w_qkv"],
        "L0_conv_w_dw": _L0_conv_in["w_dw"],
        "L0_conv_w_pw": _L0_conv_in["w_pw"],
        "L0_conv_w_proj": _L0_conv_in["w_proj"],
        "L1_conv_qkv_w": _L1_conv_in["qkv_w"],
        "L1_conv_out_w": _L1_conv_in["out_w"],
        "L1_conv_proj_lw": _L1_conv_in["proj_lw"],
        "L1_conv_proj_lb": _L1_conv_in["proj_lb"],
    }

def reference(x, L0_conv_w_qkv, L0_conv_w_dw, L0_conv_w_pw, L0_conv_w_proj, L1_conv_qkv_w, L1_conv_out_w, L1_conv_proj_lw, L1_conv_proj_lb):
    import jax
    import jax.numpy as jnp
    def _L0_conv_ref(x, w_qkv, w_dw, w_pw, w_proj):
        import jax, jax.numpy as jnp
        import numpy as np
        from jax import lax
        DIM = 8
        HEADS = 32
        SCALE = 5
        EPS = 1e-15

        def _conv2d(x, w, groups=1, pad=0):
            return lax.conv_general_dilated(x, w, window_strides=(1, 1), padding=[(pad, pad), (pad, pad)], dimension_numbers=('NCHW', 'OIHW', 'NCHW'), feature_group_count=groups)
        B, C, H, W = x.shape
        td = HEADS * DIM
        qkv = _conv2d(x, w_qkv)
        agg = _conv2d(qkv, w_dw, groups=3 * td, pad=SCALE // 2)
        agg = _conv2d(agg, w_pw, groups=3 * HEADS)
        ms = jnp.concatenate([qkv, agg], axis=1)
        ms = ms.reshape(B, -1, 3 * DIM, H * W).transpose(0, 1, 3, 2)
        q, k, v = jnp.split(ms, 3, axis=-1)
        q = jax.nn.relu(q)
        k = jax.nn.relu(k)
        v = jnp.pad(v, ((0, 0), (0, 0), (0, 0), (0, 1)), constant_values=1.0)
        kv = jnp.einsum('bgnd,bgne->bgde', k, v)
        out = jnp.einsum('bgnd,bgde->bgne', q, kv)
        out = out[..., :-1] / (out[..., -1:] + EPS)
        out = out.transpose(0, 1, 3, 2).reshape(B, -1, H, W)
        return _conv2d(out, w_proj)

    def _L1_conv_ref(x, qkv_w, out_w, proj_lw, proj_lb):
        import jax, jax.numpy as jnp
        import numpy as np
        B, C, H, W = (8, 256, 64, 64)
        NH, D = (4, 64)
        BLKQ = BLKK = 64
        TOPK_RATIO = 0.1
        EPS = 1e-06

        def _sla_forward(x, qkv_w, out_w, proj_lw, proj_lb):
            Bn, Cn, Hn, Wn = x.shape
            L = Hn * Wn
            nQ, nK = (L // BLKQ, L // BLKK)
            T = max(1, int(TOPK_RATIO * nK))
            xf = x.reshape(Bn, Cn, L)
            qkv = jnp.einsum('oc,bcl->bol', qkv_w, xf)
            q, k, v = jnp.split(qkv, 3, axis=1)

            def to_bhld(t):
                return t.reshape(Bn, NH, D, L).transpose(0, 1, 3, 2)
            q, k, v = (to_bhld(q), to_bhld(k), to_bhld(v))
            qr = q.reshape(Bn, NH, nQ, BLKQ, D)
            kr = k.reshape(Bn, NH, nK, BLKK, D)
            vr = v.reshape(Bn, NH, nK, BLKK, D)
            qb = qr.mean(axis=3)
            kb = kr.mean(axis=3)
            blk_scores = jnp.einsum('bhnd,bhmd->bhnm', qb, kb)
            _, lut = jax.lax.top_k(blk_scores, T)
            idx = lut[..., None, None]
            kg = jnp.take_along_axis(kr[:, :, None], idx, axis=3)
            vg = jnp.take_along_axis(vr[:, :, None], idx, axis=3)
            kg = kg.reshape(Bn, NH, nQ, T * BLKK, D)
            vg = vg.reshape(Bn, NH, nQ, T * BLKK, D)
            scale = D ** (-0.5)
            s = jnp.einsum('bhnqd,bhnkd->bhnqk', qr, kg) * scale
            p = jax.nn.softmax(s, axis=-1)
            o_s = jnp.einsum('bhnqk,bhnkd->bhnqd', p, vg)
            c_q = jax.nn.softmax(q, axis=-1)
            c_k = jax.nn.softmax(k, axis=-1)
            c_kr = c_k.reshape(Bn, NH, nK, BLKK, D)
            kvb = jnp.einsum('bhmkd,bhmke->bhmde', c_kr, vr)
            ksum = c_kr.sum(axis=3)
            sel = jax.nn.one_hot(lut, nK, dtype=q.dtype).sum(axis=3)
            comp = 1.0 - sel
            kv_q = jnp.einsum('bhnm,bhmde->bhnde', comp, kvb)
            ks_q = jnp.einsum('bhnm,bhmd->bhnd', comp, ksum)
            c_qr = c_q.reshape(Bn, NH, nQ, BLKQ, D)
            num = jnp.einsum('bhnqd,bhnde->bhnqe', c_qr, kv_q)
            den = jnp.einsum('bhnqd,bhnd->bhnq', c_qr, ks_q)
            o_l = num / (den[..., None] + EPS)
            o_l = jnp.einsum('bhnqd,ed->bhnqe', o_l, proj_lw) + proj_lb
            o = (o_s + o_l).reshape(Bn, NH, L, D)
            o = o.transpose(0, 1, 3, 2).reshape(Bn, Cn, L)
            o = jnp.einsum('oc,bcl->bol', out_w, o)
            return o.reshape(Bn, Cn, Hn, Wn)
        return _sla_forward(x, qkv_w, out_w, proj_lw, proj_lb)

    def _gn(v, G=32, eps=1e-5):
        B_, C_, H_, W_ = v.shape
        g = v.reshape(B_, G, C_ // G, H_, W_)
        m = jnp.mean(g, axis=(2, 3, 4), keepdims=True)
        s = jnp.var(g, axis=(2, 3, 4), keepdims=True)
        return ((g - m) / jnp.sqrt(s + eps)).reshape(v.shape)

    def _ln_c(v, eps=1e-6):
        m = jnp.mean(v, axis=1, keepdims=True)
        s = jnp.var(v, axis=1, keepdims=True)
        return (v - m) / jnp.sqrt(s + eps)

    def _ln_t(v, eps=1e-5):
        m = jnp.mean(v, axis=-1, keepdims=True)
        s = jnp.var(v, axis=-1, keepdims=True)
        return (v - m) / jnp.sqrt(s + eps)

    def _to_tokens(v):
        B_, C_, H_, W_ = v.shape
        return v.reshape(B_, C_, H_ * W_).transpose(0, 2, 1)
    def _from_tokens(t, like):
        B_, C_, H_, W_ = like.shape
        return t.transpose(0, 2, 1).reshape(B_, C_, H_, W_)

    x = x + _L0_conv_ref(_gn(x), L0_conv_w_qkv, L0_conv_w_dw, L0_conv_w_pw, L0_conv_w_proj)
    x = x + _L1_conv_ref(_gn(x), L1_conv_qkv_w, L1_conv_out_w, L1_conv_proj_lw, L1_conv_proj_lb)
    return x


_drawn_inputs = setup_inputs


def setup_inputs(seed=0):
    import zlib

    import numpy as np

    out = dict(_drawn_inputs(seed))
    spreads = {}
    factors = {'L0_conv_w_dw': 7.886,
     'L0_conv_w_pw': 7.139,
     'L1_conv_proj_lw': 8.0,
     'L1_conv_proj_lb': 3.099}
    for name, (base, spread) in spreads.items():
        noise = np.random.default_rng([zlib.crc32(name.encode()), seed]).standard_normal(out[name].shape)
        drawn = base * np.exp(spread * noise) if base else spread * noise
        out[name] = jnp.asarray(drawn.astype(out[name].dtype))
    for name, factor in factors.items():
        out[name] = (out[name] * factor).astype(out[name].dtype)
    return out
```

```python
from contextlib import ExitStack

import concourse.bass as bass
from concourse import mybir

F32 = mybir.dt.float32
I32 = mybir.dt.int32
U32 = mybir.dt.uint32
ALU = mybir.AluOpType
ACT = mybir.ActivationFunctionType
AX = mybir.AxisListType

P = 128
C, HH, WW = 256, 64, 64
L = HH * WW
KT = C // P
PL, R = 16, 16
PW = R + 1
PAD = PW * PW
CH = 512
NCH = L // CH
NH, D = 4, 64
NBLK = L // D
TOPK = 6
D1 = D + 1
KVW = D + 2 * D1
GN_EPS, ATT_EPS, LIN_EPS = 1e-5, 1e-15, 1e-6

I_QKV, I_CK, I_CV, I_SUM0, I_CQ, I_SUM1, I_ATT0, I_ATT1, I_PROJ, HALF_ITEMS = 0, 24, 32, 40, 58, 66, 82, 98, 114, 130
L0_ITEMS = 2 * HALF_ITEMS
D_ITEMS = KT * NCH
ITEMS = L0_ITEMS + 2 * D_ITEMS
IT = ITEMS // 2
SUM_ITEMS = (18, 16)
PAIRS = 48
PARTS = (1, 2, 0)
TAPS = 72
TP = 16
XADDS = 32


def conv_item(n):
    g, m = n // 24, n % 24
    return g * HALF_ITEMS + (I_CK, I_CV, I_CQ)[m // 8] + m % 8


def count(i, e):
    return (i - e) // 2 + 1


class Order:

    def __init__(self, eng, sem, base, total):
        self.eng, self.sem, self.base, self.total, self.n = eng, sem, base, total, 0

    def after(self, ins):
        self.n += 1
        ins.then_inc(self.sem, 1)
        self.eng.wait_ge(self.sem, self.base + self.n)

    def close(self):
        assert self.n == self.total, (self.n, self.total)


def build(nc, x, w0, taps, wp, w1, wo, lw, lb, consts, out, n_batch):
    with ExitStack() as ctx:
        def sb(name, shape, dt=F32):
            return ctx.enter_context(nc.sbuf_tensor(name, shape, dt))

        def sem(name):
            return ctx.enter_context(nc.semaphore(name))

        W0 = sb("W0", [P, KT, 3 * C])
        WP = sb("WP", [P, 4, C])
        W1 = sb("W1", [P, KT, NH, 3 * D])
        WO = sb("WO", [P, NH, C])
        CST = sb("CST", [P, 2 * P + 4])
        ident, same8 = CST[:, 0:P], CST[:, P:2 * P]
        HALVES = CST[:, 2 * P:2 * P + 2]
        QSC = CST[:, 2 * P + 3:2 * P + 4]
        EPSV = CST[:, 2 * P + 2:2 * P + 3]
        SMALL = 192
        SM = sb("SM", [P, SMALL])
        X = sb("X", [P, KT, L])
        XN = sb("XN", [P, KT, L])
        ARENA = 31098
        arena = sb("arena", [P, ARENA])
        PS = ctx.enter_context(nc.psum_tensor("PS", [P, 8, CH], F32))

        class Region:
            def __init__(self, tensor, size):
                self.t, self.size, self.at = tensor, size, 0

            def take(self, n):
                self.at += n
                assert self.at <= self.size, (self.at, self.size)
                return self.t[:, self.at - n:self.at]

        small = Region(SM, SMALL)
        STATS = small.take(KT * 8 * 6).rearrange("p (k c s) -> p k c s", k=KT, c=8)
        MV = small.take(2 * KT)
        GM = small.take(2 * KT)
        DEV = small.take(KT)
        SQ = small.take(KT)
        VAR = small.take(KT)
        STD = small.take(KT)
        RSTD = small.take(KT)
        NBIAS = small.take(KT)
        KSUM = small.take(2)
        BIAS = small.take(KT)
        LB = small.take(1)
        MX = small.take(8)
        SU = small.take(8)
        RC = small.take(8)
        NM = small.take(2)
        DNQ = small.take(4)
        RNQ = small.take(4)
        MX8 = small.take(8 * NH)

        l0 = Region(arena, ARENA)
        RAW = [l0.take(PL * PAD) for _ in range(3)]
        AGG = [RAW[1][:, 0:L], l0.take(L), l0.take(L)]
        IN = [l0.take(2 * PAD) for _ in range(3)]
        OUTG = [l0.take(2 * 256) for _ in range(3)]
        TW = [l0.take(2 * CH) for _ in range(2)]
        DW = [l0.take(8 * TAPS) for _ in range(2)]
        KTS = [l0.take(2 * P) for _ in range(2)]
        VTS = [l0.take(2 * (P + 1)) for _ in range(2)]
        WN, WD = [l0.take(P) for _ in range(2)], [l0.take(P) for _ in range(2)]
        DN = [l0.take(CH) for _ in range(2)]
        ADD0 = DN

        l1 = Region(arena, ARENA)
        KVB = l1.take(NBLK * KVW)
        kvb = KVB.rearrange("p (m n) -> p m n", m=NBLK)
        QS = l1.take(L)
        OT = l1.take(2 * L)
        VN = [l1.take(8 * D1) for _ in range(2)]
        QBD = [l1.take(4 * P) for _ in range(2)]
        PR = [l1.take(TOPK * D) for _ in range(2)]
        PT = [l1.take(TOPK * D) for _ in range(2)]
        SG = [l1.take(8 * D) for _ in range(2)]
        ON = [l1.take(4 * D) for _ in range(2)]
        KVT = l1.take(D1)
        ADD1 = SG
        XBM = PR[0][:, 0:KT * NBLK].rearrange("p (k n) -> p k n", k=KT)
        QB, KB, SC = PT[0][:, 0:4 * NBLK], PT[1][:, 0:4 * NBLK], PR[1][:, 0:4 * NBLK]
        IDX = sb("IDX", [D, 8 * NH], I32)
        IU = sb("IU", [D, 8 * NH], U32)
        IDXR = l1.take(2 * 8 * NBLK)[0:1, :].bitcast(I32)

        def chunk_of(tile, c):
            f = 2 * c
            oy, ox = f // 8, (f % 4) // 2
            return tile.rearrange("p (f r c) -> p f r c", f=PL, r=PW)[:, f:f + 2, oy:oy + R, ox:ox + R]

        def raw_half(j, h):
            start = h * P + (PL * PAD - 36 * P if h >= 18 else 0)
            return RAW[j][:, start:start + P]

        def agg_half(j, h):
            return AGG[j][:, h * P:(h + 1) * P]

        def planes(ap):
            return ap.rearrange("p (f r c) -> p f r c", f=2, r=R)

        def natural(tile, fy):
            return tile.rearrange("p (r fy c fx) -> p fy fx r c", fy=4, c=R, fx=4)[:, fy]

        def x_planes(kt, c):
            f = 2 * c
            return natural(X[:, kt, :], f // 4)[:, f % 4:f % 4 + 2]

        s_w = sem("weights_loaded")
        s_wo = sem("wo_folded")
        s_bias = sem("bias_summed")
        s_ld = sem("x_loaded")
        s_st = sem("x_stored")
        s_mv = sem("channel_stats")
        s_gm = sem("group_sums")
        s_var = sem("group_variance")
        s_std = sem("group_std")
        s_rstd = sem("group_rstd")
        s_xna = sem("xn_by_act")
        s_xnd = sem("xn_by_dve")
        s_it = [sem("item_for_act"), sem("item_for_dve")]
        s_free = [sem("bank_freed_by_act"), sem("bank_freed_by_dve")]
        s_zero = sem("zeros_set")
        s_taps = [sem(f"taps_loaded{i}") for i in range(2)]
        s_tw = sem("toeplitz_built")
        s_in = [sem(f"conv_in{i}") for i in range(3)]
        s_og = [sem(f"conv_out{i}") for i in range(3)]
        s_kv = sem("kv_summed")
        s_w2 = sem("kv_weights")
        s_qr = sem("q_relu")
        s_xp = sem("x_added_by_pool")
        s_xbm = sem("block_sums")
        s_qkb = sem("block_qk")
        s_qkc = sem("block_qk_copied")
        s_sc = sem("block_scores")
        s_idx = sem("block_indices")
        s_ir = [sem(f"indices_in_row{i}") for i in range(2)]
        s_zero1 = sem("zeros_set_layer1")
        s_qp = sem("qkv_tokens")
        s_sub = sem("max_subtracted")
        s_raw = sem("qkv_copied")
        s_exp = sem("features_exp")
        s_rc = sem("feature_sums")
        s_nrm = sem("features_normalised")
        s_tb = sem("qk_turned")
        s_tbe = sem("qk_stored")
        s_vd = [sem(f"v_spread{i}") for i in range(2)]
        s_kvt = sem("kv_total")
        s_qbd = sem("q_block_diagonal")
        s_s = sem("scores")
        s_nm = sem("scores_max")
        s_p = sem("scores_exp")
        s_t = sem("probs_turned")
        s_pt = sem("probs_stored")
        s_o = sem("attended")
        s_on = sem("normalised")
        s_ont = sem("outputs_turned")
        s_one = sem("outputs_stored")
        s_settled = sem("settled")
        s_dve = sem("dve_order")
        s_dveb = sem("dve_order_tokens")
        s_dvec = sem("dve_order_attention")

        block = ctx.enter_context(nc.Block())

        def wait_emptied(eng, b, i):
            for e in range(2):
                eng.wait_ge(s_free[e], b * IT + 2 + count(i, e))

        def wait_filled(eng, b, i):
            eng.wait_ge(s_it[i % 2], b * IT + count(i, i % 2))

        def settle(eng):
            eng.sem_inc(s_settled, 1)

        @block.sync
        def _(sp):
            for dst, src in ((W0[:], w0), (WP[:], wp), (W1[:], w1), (WO[0:D], wo), (CST[:], consts),
                             (arena[0:D, 0:P], lw), (LB[0:D, :], lb)):
                sp.dma_start(dst, src).then_inc(s_w, 16)
            sp.sem_inc(s_st, 16)
            for s in s_og:
                sp.sem_inc(s, 32)
            with sp.Fori(0, n_batch) as b:
                sp.wait_ge(s_st, b * 32 + 16)
                for kt in range(KT):
                    sp.dma_start(X[:, kt, :], x[bass.ds(b, 1), kt].rearrange("o p n -> (o p) n")).then_inc(s_ld, 16)

                def load_taps(t):
                    if t >= 2:
                        sp.wait_ge(s_tw, b * PAIRS + 4 * (t - 1))
                    g, j, hf = t // 6, PARTS[t % 6 // 2], t % 2
                    sp.dma_start(DW[t % 2], taps[j * 2 + g, hf]).then_inc(s_taps[t % 2], 16)

                def load_pair(n):
                    g, j, pr = n // 24, PARTS[n % 24 // 8], n % 8
                    if n % 4 == 0 and 1 <= n // 4 <= 10:
                        load_taps(n // 4 + 1)
                    if n >= 3:
                        wait_filled(sp, b, conv_item(n - 3))
                    if pr == 0:
                        settle(sp)
                        wait_emptied(sp, b, g * HALF_ITEMS + I_QKV + 8 * j + 7)
                    for a in range(2):
                        ch = 8 * (2 * pr + a)
                        sp.dma_start(IN[n % 3][:, a * PAD:(a + 1) * PAD],
                                     RAW[j][ch:ch + 8, :].rearrange("p (f n) -> p f n", f=PL)
                                     ).then_inc(s_in[n % 3], 16)

                def store_pair(n):
                    j, pr = PARTS[n % 24 // 8], n % 8
                    i = conv_item(n)
                    sp.wait_ge(s_free[i % 2], b * IT + 2 + count(i, i % 2))
                    for a in range(2):
                        ch = 8 * (2 * pr + a)
                        sp.dma_start(AGG[j][ch:ch + 8, :].rearrange("p (f n) -> p f n", f=PL),
                                     OUTG[n % 3][:, a * 256:(a + 1) * 256]).then_inc(s_og[n % 3], 16)

                load_taps(0)
                load_taps(1)
                for g in range(2):
                    for k in range(24 + 2):
                        if k < 24:
                            load_pair(24 * g + k)
                        if k >= 2:
                            store_pair(24 * g + k - 2)
                sp.wait_ge(s_idx, b + 1)
                sp.wait_ge(s_zero1, b + 1)
                for hp in range(2):
                    if hp == 1:
                        sp.wait_ge(s_one, b * 64 + 32)
                    for hl in range(2):
                        h = 2 * hp + hl
                        sp.dma_start(IDXR[:, hl * 8 * NBLK:(hl + 1) * 8 * NBLK].rearrange("o (n k) -> o n k", k=8),
                                     IDX[:, 8 * h:8 * h + 8]).then_inc(s_ir[hl], 16)
                    with sp.Fori(0, 2) as hl:
                        hd = b * NH + 2 * hp + hl
                        for gr in range(4):
                            sp.wait_ge(s_raw, hd * TP + 4 * (gr + 1))
                            v = VN[gr % 2].rearrange("p (t n) -> p t n", t=8)[:, :, 0:D]
                            blocks = kvb.rearrange("p (t u) n -> p t u n", u=2)[:, 8 * gr:8 * gr + 8]
                            for u in range(2):
                                for half in range(2):
                                    col = D + D1 * half
                                    sp.dma_start(blocks[D * half:D * (half + 1), :, u, col:col + D],
                                                 v[D * u:D * (u + 1)]).then_inc(s_vd[gr % 2], 16)
                sp.wait_ge(s_xp, (b + 1) * XADDS)
                settle(sp)
                sp.wait_ge(s_free[1], b * IT + 2 + count(ITEMS - 1, 1))
                for kt in range(KT):
                    sp.dma_start(out[bass.ds(b, 1), kt].rearrange("o p n -> (o p) n"), X[:, kt, :]).then_inc(s_st, 16)
            sp.wait_ge(s_st, 32 * n_batch + 16)

        @block.gpsimd
        def _(pool):
            pool.wait_ge(s_bias, 2)
            with pool.Fori(0, n_batch) as b:
                pool.wait_ge(s_ld, (b + 1) * 32)
                settle(pool)
                for j in range(3):
                    pool.memset(RAW[j], 0.0).then_inc(s_zero, 1)
                for s in range(2):
                    pool.memset(VTS[s].rearrange("p (u n) -> p u n", u=2)[:, :, P:P + 1], 1.0).then_inc(s_zero, 1)

                def toeplitz(n):
                    t = n // 4
                    if n % 4 == 0:
                        pool.wait_ge(s_taps[t % 2], b * 96 + 16 * (t // 2 + 1))
                    if n >= 2:
                        wait_filled(pool, b, conv_item(n - 2))
                    dw = DW[t % 2].rearrange("p (h n) -> p h n", h=8)
                    for a in range(2):
                        hh = 2 * (n % 4) + a
                        o = TW[n % 2][:, a * CH:(a + 1) * CH].rearrange("p (k c q) -> p k c q", k=4, c=8)
                        tap = dw[:, hh, 0:64].rearrange("p (k q) -> p k q", k=4)
                        tap = tap.unsqueeze(2).broadcast_to([P, 4, 8, 16])
                        mix = dw[:, hh, 64:72].unsqueeze(1).unsqueeze(3).broadcast_to([P, 4, 8, 16])
                        last = pool.tensor_tensor(o, tap, mix, ALU.mult)
                    last.then_inc(s_tw, 1)

                def add_to_x(n, i, buf, target):
                    pool.wait_ge(s_free[0], b * IT + 2 + count(i, 0))
                    pool.tensor_tensor(target, target, buf, ALU.add).then_inc(s_xp, 1)

                for g in range(2):
                    for n in range(24 * g, 24 * g + 24):
                        toeplitz(n)
                    for k in range(3):
                        pool.wait_ge(s_in[k], b * 512 + 256 * (g + 1))
                    settle(pool)
                    pool.tensor_scalar(RAW[0], RAW[0], 0.0, None, ALU.max).then_inc(s_qr, 1)
                    for k in range(8):
                        add_to_x(8 * g + k, g * HALF_ITEMS + I_PROJ + 2 * k, planes(ADD0[k % 2]),
                                 x_planes(2 * k // 8, 2 * k % 8))
                    if g == 0:
                        wait_filled(pool, b, HALF_ITEMS - 1)
                        settle(pool)
                        pool.memset(RAW[1], 0.0).then_inc(s_zero, 1)
                wait_filled(pool, b, L0_ITEMS - 1)
                settle(pool)
                for half in range(2):
                    col = D + D1 * half + D
                    pool.memset(kvb[:, :, col - D:col], 0.0)
                    pool.tensor_copy(kvb[:, :, col:col + 1], HALVES[:, half:half + 1].unsqueeze(1)
                                     .broadcast_to([P, NBLK, 1]))
                pool.memset(KVT, 0.0)
                for s in range(2):
                    last = pool.memset(VN[s].rearrange("p (t n) -> p t n", t=8)[:, :, D:D1], 1.0)
                last.then_inc(s_zero1, 1)
                for hp in range(2):
                    with pool.Fori(0, 2) as hl:
                        hd = b * NH + 2 * hp + hl
                        for p in range(TP):
                            sg = SG[p % 2].rearrange("p (u s d) -> p u s d", u=2, s=4)
                            feat = sg[:, :, 1:4:2, :]
                            rc = RC[:, 4 * (p % 2):4 * (p % 2) + 4].rearrange("p (u s) -> p u s", u=2)
                            pool.wait_ge(s_rc, hd * TP + p + 1)
                            pool.tensor_tensor(feat, feat, rc.unsqueeze(3).broadcast_to([P, 2, 2, D]),
                                               ALU.mult).then_inc(s_nrm, 1)
                        pool.wait_ge(s_tbe, (hd + 1) * TP)
                        settle(pool)

                        def spread_q(quad, s):
                            src = QS[:, bass.ds(quad * 4 * D, 4 * D)].rearrange("p (n c) -> p n c", n=4)
                            pool.tensor_tensor(QBD[s].rearrange("p (n h c) -> p n h c", n=4, h=2),
                                               src.unsqueeze(2).broadcast_to([P, 4, 2, D]),
                                               HALVES.unsqueeze(1).unsqueeze(3).broadcast_to([P, 4, 2, D]),
                                               ALU.mult).then_inc(s_qbd, 1)

                        spread_q(0, 0)
                        spread_q(1, 1)
                        with pool.Fori(1, 8) as qq:
                            for s in range(2):
                                pool.wait_ge(s_o, hd * 16 + 2 * qq + (s - 1))
                                settle(pool)
                                spread_q(2 * qq + s, s)
                    for k in range(8):
                        i = 2 * k
                        add_to_x(16 + 8 * hp + k, L0_ITEMS + D_ITEMS * hp + i, ADD1[k % 2],
                                 X[:, i // 8, (i % 8) * CH:(i % 8 + 1) * CH])

        @block.tensor
        def _(pe):
            pe.wait_ge(s_w, 16 * 7)
            for h in range(NH):
                last = nc.tensor.matmul(PS[:, h // 2, (h % 2) * C:(h % 2 + 1) * C], lhsT=arena[0:D, 0:P],
                                        rhs=WO[0:D, h, :], start=True, stop=True)
            last.then_inc(s_wo, 1)
            for ot in range(KT):
                for h in range(NH):
                    last = nc.tensor.matmul(PS[:, 2 + ot, 0:1], lhsT=WO[0:D, h, ot * P:(ot + 1) * P],
                                            rhs=LB[0:D, :], start=(h == 0), stop=(h == NH - 1))
            last.then_inc(s_wo, 1)
            pe.wait_ge(s_bias, 2)
            LAST = (NBLK - 1) * KVW
            regs = [[pe.alloc_register(f"offset{s}_{j}") for j in range(TOPK)] for s in range(4)]
            with pe.Fori(0, n_batch) as b:
                def bank(i):
                    return PS[:, i % 4, :]

                def claim(i):
                    pe.wait_ge(s_free[i % 2], b * IT + i // 2 + 1)

                def hand(i, ins):
                    ins.then_inc(s_it[i % 2], 1)

                def group_sums(layer):
                    for k in range(2):
                        pe.wait_ge(s_mv, b * 4 + 2 * layer + 1 + k)
                        nc.tensor.matmul(PS[:, 6, 8 * k:8 * k + (4, 2)[k]], lhsT=same8, rhs=(MV, SQ)[k],
                                         start=True, stop=True).then_inc(s_gm, 1)

                group_sums(0)
                pe.wait_ge(s_xna, b * 8 + 4)
                pe.wait_ge(s_xnd, b * 8 + 4)
                for g in range(2):
                    base = g * HALF_ITEMS

                    def conv(i0, n0):
                        for pr in range(8):
                            i, n = i0 + pr, n0 + pr
                            claim(i)
                            pe.wait_ge(s_tw, b * PAIRS + n + 1)
                            pe.wait_ge(s_in[n % 3], b * 512 + 32 * (n // 3 + 1))
                            for a in range(2):
                                src = IN[n % 3][:, a * PAD:(a + 1) * PAD].rearrange("p (r c) -> p r c", r=PW)
                                for k in range(4):
                                    last = nc.tensor.matmul(
                                        bank(i)[:, a * 256:(a + 1) * 256],
                                        lhsT=TW[n % 2][:, a * CH + k * P:a * CH + (k + 1) * P],
                                        rhs=src[:, k // 2:k // 2 + R, k % 2:k % 2 + R],
                                        start=(k == 0), stop=(k == 3))
                            hand(i, last)

                    def kv_sums(src, half, i0):
                        n_items = SUM_ITEMS[src]

                        def add_up(t):
                            i = i0 + t
                            pe.wait_ge(s_free[i % 2], b * IT + 2 + count(i, i % 2))
                            for u in range(2):
                                last = nc.tensor.matmul(PS[:, 4 + src, 0:P + 1], lhsT=KTS[t % 2][:, u * P:(u + 1) * P],
                                                        rhs=VTS[t % 2][:, u * (P + 1):(u + 1) * (P + 1)],
                                                        start=(t == 0 and u == 0), stop=(t == n_items - 1 and u == 1))
                            if t == n_items - 1:
                                last.then_inc(s_kv, 1)
                        for t in range(n_items):
                            claim(i0 + t)
                            for u in range(2):
                                nc.tensor.transpose(bank(i0 + t)[:, u * P:(u + 1) * P], half(1, 2 * t + u), ident)
                                last = nc.tensor.transpose(bank(i0 + t)[:, (2 + u) * P:(3 + u) * P],
                                                           half(2, 2 * t + u), ident)
                            hand(i0 + t, last)
                            if t >= 1:
                                add_up(t - 1)
                        add_up(n_items - 1)

                    def attend(src, i0):
                        pe.wait_ge(s_w2, b * 4 + 2 * g + src + 1)
                        for c in range(NCH):
                            q = chunk_of(RAW[0], c) if src == 0 else AGG[0][:, c * CH:(c + 1) * CH]
                            for i, w in ((i0 + 2 * c, WD[src]), (i0 + 2 * c + 1, WN[src])):
                                claim(i)
                                hand(i, nc.tensor.matmul(bank(i), lhsT=w, rhs=q, start=True, stop=True))

                    def wait_stored(n):
                        for k in range(3):
                            pe.wait_ge(s_og[k], b * 512 + 32 * ((n - k) // 3 + 2))

                    for j in range(3):
                        for c in range(NCH):
                            i = base + I_QKV + 8 * j + c
                            claim(i)
                            for kt in range(KT):
                                last = nc.tensor.matmul(bank(i), lhsT=W0[:, kt, (2 * j + g) * P:(2 * j + g + 1) * P],
                                                        rhs=XN[:, kt, c * CH:(c + 1) * CH],
                                                        start=(kt == 0), stop=(kt == KT - 1))
                            hand(i, last)
                    conv(base + I_CK, 24 * g)
                    conv(base + I_CV, 24 * g + 8)
                    wait_emptied(pe, b, base + I_QKV + 23)
                    kv_sums(0, raw_half, base + I_SUM0)
                    conv(base + I_CQ, 24 * g + 16)
                    wait_stored(24 * g + 15)
                    kv_sums(1, agg_half, base + I_SUM1)
                    pe.wait_ge(s_qr, b * 2 + g + 1)
                    attend(0, base + I_ATT0)
                    wait_stored(24 * g + 23)
                    attend(1, base + I_ATT1)
                    wait_emptied(pe, b, base + I_PROJ - 1)
                    for ot in range(KT):
                        for c in range(NCH):
                            i = base + I_PROJ + NCH * ot + c
                            claim(i)
                            nc.tensor.matmul(bank(i), lhsT=WP[:, g, ot * P:(ot + 1) * P], rhs=chunk_of(RAW[0], c),
                                             start=True, stop=False)
                            hand(i, nc.tensor.matmul(bank(i), lhsT=WP[:, 2 + g, ot * P:(ot + 1) * P],
                                                     rhs=AGG[0][:, c * CH:(c + 1) * CH], start=False, stop=True))

                group_sums(1)
                pe.wait_ge(s_xbm, b + 1)
                for h in range(NH):
                    for part in range(2):
                        for kt in range(KT):
                            last = nc.tensor.matmul(PS[0:D, 5 + part, h * NBLK:(h + 1) * NBLK],
                                                    lhsT=W1[:, kt, h, part * D:(part + 1) * D], rhs=XBM[:, kt, :],
                                                    start=(kt == 0), stop=(kt == KT - 1))
                last.then_inc(s_qkb, 1)
                pe.wait_ge(s_qkc, b + 1)
                settle(pe)
                for h in range(NH):
                    cols = slice(h * NBLK, (h + 1) * NBLK)
                    last = nc.tensor.matmul(PS[0:D, 7, cols], lhsT=QB[0:D, cols], rhs=KB[0:D, cols],
                                            start=True, stop=True)
                last.then_inc(s_sc, 1)
                pe.wait_ge(s_sc, b + 1)
                pe.wait_ge(s_zero1, b + 1)
                pe.wait_ge(s_idx, b + 1)
                for hp in range(2):
                    wait_emptied(pe, b, L0_ITEMS + D_ITEMS * hp - 1)
                    settle(pe)
                    with pe.Fori(0, 2) as hl:
                        hd = b * NH + 2 * hp + hl

                        def turn(p):
                            pe.wait_ge(s_nrm, hd * TP + p + 1)
                            if p >= 2:
                                pe.wait_ge(s_tbe, hd * TP + p - 1)
                            sg = SG[p % 2]
                            vn = VN[p // 4 % 2]
                            for u in range(2):
                                k_ck = sg[:, (4 * u + 2) * D:(4 * u + 4) * D]
                                nc.tensor.transpose(PS[:, 2 + p % 2, u * P:(u + 1) * P],
                                                    sg[:, 4 * u * D:(4 * u + 2) * D], ident)
                                nc.tensor.transpose(PS[:, 2 + p % 2, (2 + u) * P:(3 + u) * P], k_ck, ident)
                            for u in range(2):
                                t = 2 * (p % 4) + u
                                last = nc.tensor.matmul(PS[:, 7, 0:D1], lhsT=sg[:, (4 * u + 2) * D:(4 * u + 4) * D],
                                                        rhs=vn[:, t * D1:(t + 1) * D1],
                                                        start=(p == 0 and u == 0), stop=(p == TP - 1 and u == 1))
                            last.then_inc(s_tb, 1)

                        for p in range(TP):
                            if p >= 2:
                                pe.wait_ge(s_raw, hd * TP + p - 1)
                            for u in range(2):
                                t = 2 * p + u
                                for kt in range(KT):
                                    last = nc.tensor.matmul(
                                        PS[:, p % 2, u * 3 * D:(u + 1) * 3 * D], lhsT=XN[:, kt, t * P:(t + 1) * P],
                                        rhs=W1[:, kt, bass.ds(2 * hp + hl, 1), :].rearrange("p o n -> p (o n)"),
                                        start=(kt == 0), stop=(kt == KT - 1))
                            last.then_inc(s_qp, 1)
                            if p >= 1:
                                turn(p - 1)
                        turn(TP - 1)
                        pe.wait_ge(s_tbe, (hd + 1) * TP)
                        for k in range(2):
                            pe.wait_ge(s_vd[k], (hd + 1) * 128)
                        pe.wait_ge(s_kvt, hd + 1)
                        for k in range(2):
                            pe.wait_ge(s_ir[k], (b * 2 + hp + 1) * 16)

                        taken = {}

                        def offsets(u8):
                            return [pe.snap(r, min_val=0, max_val=LAST) for r in regs[u8 % 4]]

                        def turn_probs(nb, u):
                            pe.wait_ge(s_p, nb + (u + 1))
                            u8 = u % 8
                            for j in range(3):
                                last = nc.tensor.transpose(PS[:, 2 + u8 % 2, j * P:(j + 1) * P],
                                                           PR[u8 % 2][:, j * P:(j + 1) * P], ident)
                            last.then_inc(s_t, 1)

                        def apply(nb, u):
                            pe.wait_ge(s_pt, nb + (u + 1))
                            u8 = u % 8
                            off = taken.pop(u, None) or offsets(u8)
                            o = PS[:, 4 + u8 // 4, (u8 % 4) * D1:(u8 % 4 + 1) * D1]
                            nc.tensor.matmul(o, lhsT=QBD[u8 // 4][:, (u8 % 4) * P:(u8 % 4 + 1) * P], rhs=KVT,
                                             start=True, stop=False)
                            for j in range(TOPK):
                                last = nc.tensor.matmul(o, lhsT=PT[u8 % 2][:, (j // 2) * P:(j // 2 + 1) * P],
                                                        rhs=KVB[:, bass.ds(off[j] + (D + D1 * (j % 2)), D1)],
                                                        start=False, stop=(j == TOPK - 1))
                            if u8 % 4 == 3:
                                last.then_inc(s_o, 1)

                        def turn_out(quad, s):
                            pe.wait_ge(s_on, hd * 16 + quad + 1)
                            if not isinstance(quad, int) or quad > 0:
                                pe.wait_ge(s_one, hd * 16 + quad)
                            for k in range(2):
                                last = nc.tensor.transpose(PS[:, 6, (2 * s + k) * P:(2 * s + k + 1) * P],
                                                           ON[s][:, k * P:(k + 1) * P], ident)
                            last.then_inc(s_ont, 1)

                        def step(nb, row, u8, first, quad):
                            if u8 % 4 == 0:
                                pe.wait_ge(s_qbd, hd * 16 + quad + 1)
                            pe.load(regs[u8 % 4], IDXR[:, bass.ds(row + 8 * u8, TOPK)])
                            off = taken[u8] = offsets(u8)
                            q = QBD[u8 // 4][:, (u8 % 4) * P:(u8 % 4 + 1) * P]
                            for j in range(TOPK):
                                last = nc.tensor.matmul(PS[:, u8 % 2, j * D:(j + 1) * D], lhsT=q,
                                                        rhs=KVB[:, bass.ds(off[j], D)], start=True, stop=True)
                            last.then_inc(s_s, 1)
                            if not (first and u8 < 1):
                                turn_probs(nb, u8 - 1)
                            if not (first and u8 < 2):
                                apply(nb, u8 - 2)
                            if u8 % 4 == 3 and not (first and u8 == 3):
                                turn_out(quad - 1, (u8 // 4 + 1) % 2)

                        nb = pe.snap(hd * NBLK)
                        row = pe.snap(hl * (8 * NBLK))
                        for u8 in range(8):
                            step(nb, row, u8, True, u8 // 4)
                        taken.clear()
                        with pe.Fori(1, 8) as qq:
                            nb = pe.snap(hd * NBLK + 8 * qq)
                            row = pe.snap(hl * (8 * NBLK) + 8 * 8 * qq)
                            for u8 in range(8):
                                step(nb, row, u8, False, 2 * qq + u8 // 4)
                        taken.clear()
                        nb = hd * NBLK + NBLK
                        turn_probs(nb, -1)
                        apply(nb, -2)
                        apply(nb, -1)
                        turn_out(15, 1)
                        pe.wait_ge(s_one, hd * 16 + 16)
                    for ot in range(KT):
                        for c in range(NCH):
                            i = L0_ITEMS + D_ITEMS * hp + NCH * ot + c
                            claim(i)
                            for hh in range(2):
                                last = nc.tensor.matmul(bank(i), lhsT=WO[:, 2 * hp + hh, ot * P:(ot + 1) * P],
                                                        rhs=OT[:, hh * L + c * CH:hh * L + (c + 1) * CH],
                                                        start=(hh == 0), stop=(hh == 1))
                            hand(i, last)

        def empty_half(eng, e, b, g, copy, relu, between):
            base = g * HALF_ITEMS

            def conv(i0, n0, op):
                for pr in range(8):
                    i, n = i0 + pr, n0 + pr
                    if i % 2 == e:
                        wait_filled(eng, b, i)
                        eng.wait_ge(s_og[n % 3], b * 512 + 32 * (n // 3 + 1))
                        op(OUTG[n % 3], PS[:, i % 4, :]).then_inc(s_free[e], 1)

            def turned(i0, n_items):
                for t in range(n_items):
                    i = i0 + t
                    if i % 2 == e:
                        wait_filled(eng, b, i)
                        relu(KTS[t % 2], PS[:, i % 4, 0:2 * P])
                        copy(VTS[t % 2].rearrange("p (u n) -> p u n", u=2)[:, :, 0:P],
                             PS[:, i % 4, 2 * P:4 * P].rearrange("p (u n) -> p u n", u=2)).then_inc(s_free[e], 1)

            eng.wait_ge(s_zero, b * 6 + 5 + g)
            for j in range(3):
                for c in range(NCH):
                    i = base + I_QKV + 8 * j + c
                    if i % 2 == e:
                        wait_filled(eng, b, i)
                        copy(chunk_of(RAW[j], c), planes(PS[:, i % 4, :])).then_inc(s_free[e], 1)
            conv(base + I_CK, 24 * g, copy)
            conv(base + I_CV, 24 * g + 8, copy)
            turned(base + I_SUM0, SUM_ITEMS[0])
            between(0)
            conv(base + I_CQ, 24 * g + 16, relu)
            turned(base + I_SUM1, SUM_ITEMS[1])
            between(1)

        def x_chunk(layer, i):
            if layer == 0:
                return x_planes(i // NCH, i % NCH)
            return X[:, i // NCH, (i % NCH) * CH:(i % NCH + 1) * CH]

        def norm_chunk(layer, kt, q):
            if layer == 0:
                return (XN[:, kt, :].rearrange("p (fy fx r c) -> p fy fx r c", fy=4, fx=4, r=R)[:, q],
                        natural(X[:, kt, :], q))
            cols = slice(q * L // 4, (q + 1) * L // 4)
            return XN[:, kt, cols], X[:, kt, cols]

        @block.scalar
        def _(act):
            def copy(o, i):
                return nc.scalar.activation(o, i, ACT.Copy)

            def relu(o, i):
                return nc.scalar.activation(o, i, ACT.Relu)

            act.wait_ge(s_wo, 1)
            for h in range(NH):
                last = copy(WO[D:P, h, :], PS[D:P, h // 2, (h % 2) * C:(h % 2 + 1) * C])
            last.then_inc(s_bias, 1)
            act.sem_inc(s_free[0], 2)
            with act.Fori(0, n_batch) as b:
                def normalise(layer):
                    act.wait_ge(s_var, b * 2 + layer + 1)
                    nc.scalar.activation(STD, VAR, ACT.Sqrt).then_inc(s_std, 1)
                    act.wait_ge(s_rstd, b * 2 + layer + 1)
                    for q in range(4):
                        dst, src = norm_chunk(layer, 1, q)
                        nc.scalar.activation(dst, src, ACT.Identity, bias=NBIAS[:, 1:2],
                                             scale=RSTD[:, 1:2]).then_inc(s_xna, 1)

                def chunk_for_pool(n, i, buf, bias):
                    wait_filled(act, b, i)
                    if n % 8 >= 2:
                        act.wait_ge(s_xp, b * XADDS + n - 1)
                    nc.scalar.activation(buf, PS[:, i % 4, :], ACT.Identity, bias=bias).then_inc(s_free[0], 1)

                normalise(0)
                for g in range(2):
                    empty_half(act, 0, b, g, copy, relu, lambda src: None)
                    if g:
                        act.wait_ge(s_xp, b * XADDS + 8)
                    for src, i0 in enumerate((I_ATT0, I_ATT1)):
                        for c in range(NCH):
                            i = g * HALF_ITEMS + i0 + 2 * c
                            wait_filled(act, b, i)
                            act.wait_ge(s_free[1], b * IT + 2 + count(i - 3, 1))
                            nc.scalar.activation(DN[c % 2], PS[:, i % 4, :], ACT.Copy,
                                                 bias=ATT_EPS).then_inc(s_free[0], 1)
                    act.wait_ge(s_free[1], b * IT + 2 + count(g * HALF_ITEMS + I_PROJ - 1, 1))
                    for k in range(8):
                        chunk_for_pool(8 * g + k, g * HALF_ITEMS + I_PROJ + 2 * k, ADD0[k % 2], 0.0)

                normalise(1)
                act.wait_ge(s_qkb, b + 1)
                copy(QB[0:D, :], PS[0:D, 5, 0:4 * NBLK])
                copy(KB[0:D, :], PS[0:D, 6, 0:4 * NBLK]).then_inc(s_qkc, 1)
                act.wait_ge(s_zero1, b + 1)
                for hp in range(2):
                    act.wait_ge(s_xp, b * XADDS + 16 + 8 * hp)
                    settle(act)
                    with act.Fori(0, 2) as hl:
                        hd = b * NH + 2 * hp + hl

                        def store_turned(p):
                            act.wait_ge(s_tb, hd * TP + p + 1)
                            copy(kvb[:, 4 * p:4 * p + 4, 0:D],
                                 PS[:, 2 + p % 2, 2 * P:4 * P].rearrange("p (m n) -> p m n", m=4))
                            nc.scalar.activation(QS[:, p * 2 * P:(p + 1) * 2 * P], PS[:, 2 + p % 2, 0:2 * P], ACT.Copy,
                                                 scale=QSC).then_inc(s_tbe, 1)

                        for p in range(TP):
                            act.wait_ge(s_qp, hd * TP + p + 1)
                            if p % 4 == 0 and p >= 8:
                                act.wait_ge(s_vd[p // 4 % 2], hd * 128 + 64 * (p // 8))
                            sg = SG[p % 2].rearrange("p (u s d) -> p u s d", u=2, s=4)
                            ps = PS[:, p % 2, 0:6 * D].rearrange("p (u s d) -> p u s d", u=2, s=3)
                            vn = VN[p // 4 % 2].rearrange("p (t n) -> p t n", t=8)
                            copy(sg[:, :, 0:4:2, :], ps[:, :, 0:2, :])
                            copy(vn[:, 2 * (p % 4):2 * (p % 4) + 2, 0:D], ps[:, :, 2, :]).then_inc(s_raw, 1)
                            act.wait_ge(s_sub, hd * TP + p + 1)
                            feat = sg[:, :, 1:4:2, :]
                            nc.scalar.activation(feat, feat, ACT.Exp).then_inc(s_exp, 1)
                            if p >= 2:
                                store_turned(p - 2)
                        store_turned(TP - 2)
                        store_turned(TP - 1)

                        def exp(nb, u8):
                            act.wait_ge(s_nm, nb + (u8 + 1))
                            nc.scalar.activation(PR[u8 % 2][0:D, :], PS[0:D, u8 % 2, 0:TOPK * D], ACT.Exp,
                                                 bias=NM[0:D, u8 % 2:u8 % 2 + 1]).then_inc(s_p, 1)

                        def store_probs(nb, u):
                            act.wait_ge(s_t, nb + (u + 1))
                            u8 = u % 8
                            copy(PT[u8 % 2], PS[:, 2 + u8 % 2, 0:TOPK * D]).then_inc(s_pt, 1)

                        nb = act.snap(hd * NBLK)
                        exp(nb, 0)
                        for u8 in range(1, 8):
                            exp(nb, u8)
                            store_probs(nb, u8 - 1)
                        with act.Fori(1, 8) as qq:
                            nb = act.snap(hd * NBLK + 8 * qq)
                            for u8 in range(8):
                                exp(nb, u8)
                                store_probs(nb, u8 - 1)
                        store_probs(hd * NBLK + NBLK, -1)
                    for k in range(8):
                        chunk_for_pool(16 + 8 * hp + k, L0_ITEMS + D_ITEMS * hp + 2 * k, ADD1[k % 2],
                                       BIAS[:, k // 4:k // 4 + 1] if hp else 0.0)

        @block.vector
        def _(dve):
            def copy(o, i):
                return nc.vector.tensor_copy(o, i)

            def relu(o, i):
                return nc.vector.tensor_scalar(o, i, 0.0, None, ALU.max)

            dve.wait_ge(s_wo, 2)
            nc.vector.tensor_copy(BIAS, PS[:, 2:4, 0]).then_inc(s_bias, 1)
            dve.sem_inc(s_free[1], 2)
            DVE_N = 2 * 6 + 4 + 4 * NCH + 3
            with dve.Fori(0, n_batch) as b:
                order = Order(dve, s_dve, b * DVE_N, DVE_N)

                def normalise(layer):
                    for kt in range(KT):
                        for c in range(8):
                            last = nc.vector.bn_stats(STATS[:, kt, c, :], X[:, kt, c * CH:(c + 1) * CH])
                    order.after(last)
                    settle(dve)
                    mv = MV.rearrange("p (k s) -> p k s", k=KT)
                    gm = GM.rearrange("p (k s) -> p k s", k=KT)
                    nc.vector.bn_aggr(mv[:, 0, :], STATS[:, 0])
                    nc.vector.bn_aggr(mv[:, 1, :], STATS[:, 1]).then_inc(s_mv, 1)
                    dve.wait_ge(s_gm, b * 4 + 2 * layer + 1)
                    order.after(nc.vector.tensor_scalar(GM, PS[:, 6, 0:2 * KT], 1.0 / 8, None, ALU.mult))
                    order.after(nc.vector.tensor_tensor(DEV, mv[:, :, 0], gm[:, :, 0], ALU.subtract))
                    nc.vector.tensor_tensor(SQ, DEV, DEV, ALU.mult).then_inc(s_mv, 1)
                    dve.wait_ge(s_gm, b * 4 + 2 * layer + 2)
                    order.after(nc.vector.scalar_tensor_tensor(out=VAR, in0=PS[:, 6, 8:8 + KT], scalar=1.0 / 8,
                                                               in1=gm[:, :, 1], op0=ALU.mult, op1=ALU.add))
                    nc.vector.tensor_scalar(VAR, VAR, GN_EPS, None, ALU.add).then_inc(s_var, 1)
                    dve.wait_ge(s_std, b * 2 + layer + 1)
                    order.after(nc.vector.reciprocal(RSTD, STD))
                    order.after(nc.vector.tensor_tensor(NBIAS, gm[:, :, 0], RSTD, ALU.mult))
                    nc.vector.tensor_scalar(NBIAS, NBIAS, -1.0, None, ALU.mult).then_inc(s_rstd, 1)
                    for q in range(4):
                        dst, src = norm_chunk(layer, 0, q)
                        nc.vector.tensor_scalar(dst, src, GM[:, 0:1], RSTD[:, 0:1], ALU.subtract,
                                                ALU.mult).then_inc(s_xnd, 1)

                dve.wait_ge(s_ld, (b + 1) * 32)
                normalise(0)
                for g in range(2):
                    def kv_weights(src):
                        dve.wait_ge(s_kv, b * 4 + 2 * g + src + 1)
                        order.after(nc.vector.tensor_copy(KSUM[:, src:src + 1], PS[:, 4 + src, P:P + 1]))
                        nc.vector.tensor_tensor(WN[src], PS[:, 4 + src, 0:P], same8, ALU.mult)
                        nc.vector.tensor_scalar(WD[src], same8, KSUM[:, src:src + 1], None,
                                                ALU.mult).then_inc(s_w2, 1)

                    empty_half(dve, 1, b, g, copy, relu, kv_weights)
                    for src, i0 in enumerate((I_ATT0, I_ATT1)):
                        for c in range(NCH):
                            i = g * HALF_ITEMS + i0 + 2 * c + 1
                            dve.wait_ge(s_free[0], b * IT + 2 + count(i - 1, 0))
                            order.after(nc.vector.reciprocal(DN[c % 2], DN[c % 2]))
                            wait_filled(dve, b, i)
                            if src == 0:
                                nc.vector.tensor_tensor(chunk_of(RAW[0], c), planes(PS[:, i % 4, :]),
                                                        planes(DN[c % 2]), ALU.mult).then_inc(s_free[1], 1)
                            else:
                                nc.vector.tensor_tensor(AGG[0][:, c * CH:(c + 1) * CH], PS[:, i % 4, :], DN[c % 2],
                                                        ALU.mult).then_inc(s_free[1], 1)
                    for k in range(8):
                        i = 2 * k + 1
                        gi = g * HALF_ITEMS + I_PROJ + i
                        wait_filled(dve, b, gi)
                        ins = nc.vector.tensor_tensor(x_chunk(0, i), planes(PS[:, gi % 4, :]), x_chunk(0, i), ALU.add)
                        ins.then_inc(s_free[1], 1)

                dve.wait_ge(s_xp, b * XADDS + 16)
                dve.wait_ge(s_free[1], b * IT + 2 + count(L0_ITEMS - 1, 1))
                normalise(1)
                dve.wait_ge(s_xna, b * 8 + 8)
                dve.wait_ge(s_xnd, b * 8 + 8)
                for kt in range(KT):
                    ins = nc.vector.tensor_reduce(XBM[:, kt, :], XN[:, kt, :].rearrange("p (m t) -> p m t", m=NBLK),
                                                  AX.X, ALU.add)
                ins.then_inc(s_xbm, 1)
                dve.wait_ge(s_sc, b + 1)
                order.after(copy(SC[0:D, :], PS[0:D, 7, 0:4 * NBLK]))
                settle(dve)
                for h in range(NH):
                    last = nc.vector.max(MX8[0:D, 8 * h:8 * h + 8], SC[0:D, h * NBLK:(h + 1) * NBLK])
                order.after(last)
                settle(dve)
                for h in range(NH):
                    last = nc.vector.max_index(IU[:, 8 * h:8 * h + 8], MX8[0:D, 8 * h:8 * h + 8],
                                               SC[0:D, h * NBLK:(h + 1) * NBLK])
                order.after(last)
                nc.vector.tensor_scalar(IDX[:], IU[:], float(KVW), None, ALU.mult).then_inc(s_idx, 1)
                for hp in range(2):
                    with dve.Fori(0, 2) as hl:
                        hd = b * NH + 2 * hp + hl
                        torder = Order(dve, s_dveb, hd * 2 * TP, 2 * TP)

                        def sums(p):
                            dve.wait_ge(s_exp, hd * TP + p + 1)
                            feat = SG[p % 2].rearrange("p (u s d) -> p u s d", u=2, s=4)[:, :, 1:4:2, :]
                            part = slice(4 * (p % 2), 4 * (p % 2) + 4)
                            torder.after(nc.vector.tensor_reduce(SU[:, part].rearrange("p (u s) -> p u s", u=2), feat,
                                                                 AX.X, ALU.add))
                            nc.vector.reciprocal(RC[:, part], SU[:, part]).then_inc(s_rc, 1)

                        for p in range(TP):
                            dve.wait_ge(s_raw, hd * TP + p + 1)
                            sg = SG[p % 2].rearrange("p (u s d) -> p u s d", u=2, s=4)
                            qk, feat = sg[:, :, 0:4:2, :], sg[:, :, 1:4:2, :]
                            mx = MX[:, 4 * (p % 2):4 * (p % 2) + 4].rearrange("p (u s) -> p u s", u=2)
                            torder.after(nc.vector.tensor_reduce(mx, qk, AX.X, ALU.max))
                            nc.vector.tensor_tensor(feat, qk, mx.unsqueeze(3).broadcast_to([P, 2, 2, D]),
                                                    ALU.subtract).then_inc(s_sub, 1)
                            if p >= 1:
                                sums(p - 1)
                        sums(TP - 1)
                        torder.close()
                        dve.wait_ge(s_tb, (hd + 1) * TP)
                        nc.vector.tensor_scalar(KVT[D:P, :], PS[D:P, 7, 0:D1], -1.0, None,
                                                ALU.mult).then_inc(s_kvt, 1)

                        def maxima(nb, u8):
                            dve.wait_ge(s_s, nb + (u8 + 1))
                            copy(PR[u8 % 2][D:P, :], PS[D:P, u8 % 2, 0:TOPK * D])
                            nc.vector.tensor_reduce(NM[0:D, u8 % 2:u8 % 2 + 1], PS[0:D, u8 % 2, 0:TOPK * D], AX.X,
                                                    ALU.max, negate=True).then_inc(s_nm, 1)

                        def normalise_out(quad, s):
                            o = PS[:, 4 + s, 0:4 * D1].rearrange("p (n c) -> p n c", n=4)
                            chain = hd * 32 + 2 * quad
                            dve.wait_ge(s_o, hd * 16 + quad + 1)
                            nc.vector.tensor_scalar(DNQ.unsqueeze(2), o[:, :, D:D1], EPSV, None,
                                                    ALU.add).then_inc(s_dvec, 1)
                            dve.wait_ge(s_dvec, chain + 1)
                            nc.vector.reciprocal(RNQ, DNQ).then_inc(s_dvec, 1)
                            dve.wait_ge(s_dvec, chain + 2)
                            on = ON[s].rearrange("p (k c) -> p k c", k=2)
                            for u in range(2):
                                for lin in range(2):
                                    rows = slice(D * lin, D * (lin + 1))
                                    last = nc.vector.tensor_tensor(
                                        on[D * u:D * (u + 1), :, D * lin:D * (lin + 1)], o[rows, u:4:2, 0:D],
                                        RNQ[rows, u:4:2].unsqueeze(2).broadcast_to([D, 2, D]), ALU.mult)
                            last.then_inc(s_on, 1)

                        def store_out(quad, s):
                            dve.wait_ge(s_ont, hd * 16 + quad + 1)
                            copy(OT[:, bass.ds(hl * L + quad * 4 * D, 4 * D)],
                                 PS[:, 6, 2 * s * P:(2 * s + 2) * P]).then_inc(s_one, 1)

                        def step(nb, u8, first, quad):
                            maxima(nb, u8)
                            if u8 % 4 == 1 and not (first and u8 <= 5):
                                store_out(quad - 2, u8 // 4)
                            if u8 % 4 == 2 and not (first and u8 == 2):
                                normalise_out(quad - 1, (u8 // 4 + 1) % 2)

                        nb = dve.snap(hd * NBLK)
                        for u8 in range(8):
                            step(nb, u8, True, u8 // 4)
                        with dve.Fori(1, 8) as qq:
                            nb = dve.snap(hd * NBLK + 8 * qq)
                            for u8 in range(8):
                                step(nb, u8, False, 2 * qq + u8 // 4)
                        store_out(14, 0)
                        normalise_out(15, 1)
                        store_out(15, 1)
                    for k in range(8):
                        i = 2 * k + 1
                        wait_filled(dve, b, L0_ITEMS + D_ITEMS * hp + i)
                        xc = x_chunk(1, i)
                        if hp == 0:
                            ins = nc.vector.tensor_tensor(xc, PS[:, i % 4, :], xc, ALU.add)
                        else:
                            ins = nc.vector.scalar_tensor_tensor(out=xc, in0=PS[:, i % 4, :],
                                                                 scalar=BIAS[:, i // NCH:i // NCH + 1], in1=xc,
                                                                 op0=ALU.add, op1=ALU.add)
                        ins.then_inc(s_free[1], 1)
                order.close()


def kernel(**inputs):
    import numpy as np
    import concourse.bacc as bacc
    from concourse.bass_utils import run_bass_kernel_spmd as run

    x = np.ascontiguousarray(inputs["x"])
    n_batch = x.shape[0]
    a = {"x": x.reshape(n_batch, KT, P, L)}
    perm = (24 * np.arange(32)[None, :, None] + 8 * np.arange(3)[:, None, None] + np.arange(8)).reshape(-1)
    w = np.asarray(inputs["L0_conv_w_qkv"])[perm, :, 0, 0]
    a["w0"] = w.T.reshape(KT, P, 3 * C).transpose(1, 0, 2)
    dw = np.asarray(inputs["L0_conv_w_dw"])[perm, 0]
    padded = np.pad(dw, ((0, 0), (3, 3), (3, 3)))
    plane = (np.arange(4) + 2) % 4
    t = 4 * np.arange(2)[None, :, None] + plane[:, None, None] - np.arange(4)[None, None, :] + 3
    tt = padded[:, t[:, :, :, None, None, None], t[None, None, None]]
    tt = tt.transpose(0, 1, 4, 2, 5, 3, 6).reshape(96, 8 * 16, 64)
    pw = np.asarray(inputs["L0_conv_w_pw"])[perm, :, 0, 0].reshape(96, 8, 8)
    pw = np.repeat(pw.transpose(0, 2, 1), 16, axis=1)
    a["taps"] = np.concatenate([tt, pw], axis=2).reshape(6, 2, 8, P, TAPS).transpose(0, 1, 3, 2, 4).reshape(
        6, 2, P, 8 * TAPS)
    a["wp"] = np.asarray(inputs["L0_conv_w_proj"])[:, :, 0, 0].T.reshape(4, P, C).transpose(1, 0, 2)
    w = np.asarray(inputs["L1_conv_qkv_w"]).reshape(3, NH, D, C)
    a["w1"] = w.transpose(3, 1, 0, 2).reshape(KT, P, NH, 3 * D).transpose(1, 0, 2, 3)
    a["wo"] = np.asarray(inputs["L1_conv_out_w"]).T.reshape(NH, D, C).transpose(1, 0, 2)
    a["lw"] = np.pad(np.asarray(inputs["L1_conv_proj_lw"]), ((0, 0), (D, 0)))
    a["lb"] = np.asarray(inputs["L1_conv_proj_lb"])[:, None]
    group = np.arange(P) // 8
    lower = np.arange(P)[:, None] >= D
    a["consts"] = np.concatenate([np.eye(P), group[:, None] == group[None, :], ~lower, lower, -LIN_EPS * lower,
                                  np.where(lower, 1.0, D ** -0.5)],
                                 axis=1).astype(np.float32)

    nc = bacc.Bacc("TRN2", target_bir_lowering=False, num_devices=1)
    arrays, args = {}, []
    for name, v in a.items():
        v = np.ascontiguousarray(v)
        arrays[f"in_{name}"] = v
        args.append(nc.dram_tensor(f"in_{name}", v.shape, mybir.dt.from_np(v.dtype), kind="ExternalInput").ap())
    out = nc.dram_tensor("out", (n_batch, KT, P, L), F32, kind="ExternalOutput").ap()
    build(nc, *args, out, n_batch)
    r = run(nc, [arrays], core_ids=[0])
    return r.results[0]["out"].reshape(n_batch, C, HH, WW)
```

```python
from contextlib import ExitStack

import concourse.bass as bass
from concourse import mybir

F32 = mybir.dt.float32
I32 = mybir.dt.int32
U32 = mybir.dt.uint32
ALU = mybir.AluOpType
ACT = mybir.ActivationFunctionType
AX = mybir.AxisListType

P = 128
C, HH, WW = 256, 64, 64
L = HH * WW
KT = C // P
PL, R = 16, 16
PW = R + 1
PAD = PW * PW
CH = 512
NCH = L // CH
NH, D = 4, 64
NBLK = L // D
TOPK = 6
D1 = D + 1
KVW = D + D1
GN_EPS, ATT_EPS, LIN_EPS = 1e-5, 1e-15, 1e-6

I_QKV, I_CK, I_CV, I_SUM0, I_CQ, I_SUM1, I_LAST, HALF_ITEMS = 0, 24, 32, 40, 58, 66, 98, 130
L0_ITEMS = 2 * HALF_ITEMS
D_ITEMS = KT * NCH
ITEMS = L0_ITEMS + 2 * D_ITEMS
IT = ITEMS // 2
SUM_ITEMS = (18, 16)
PAIRS = 48
PARTS = (1, 2, 0)
TAPS = 72
TP = 16
POOL_KEYS = (0, 2, 4, 5)
XADDS = 32


def conv_item(n):
    g, m = n // 24, n % 24
    return g * HALF_ITEMS + (I_CK, I_CV, I_CQ)[m // 8] + m % 8


def sum1_item(t):
    return I_SUM1 + 4 * (t // 2) + t % 2


def att_item(src, c):
    return I_SUM1 + 4 * c + 2 if src == 0 else I_LAST + max(2 * c, 4 * c - 4)


def proj_item(c):
    return I_LAST + min(4 * c + 6, 2 * c + 16)


def count(i, e):
    return (i - e) // 2 + 1


class Order:

    def __init__(self, eng, sem, base, total):
        self.eng, self.sem, self.base, self.total, self.n = eng, sem, base, total, 0

    def after(self, ins):
        self.n += 1
        ins.then_inc(self.sem, 1)
        self.eng.wait_ge(self.sem, self.base + self.n)

    def close(self):
        assert self.n == self.total, (self.n, self.total)


def build(nc, x, w0, taps, wp, w1, wo, lw, lb, consts, out, n_batch):
    with ExitStack() as ctx:
        def sb(name, shape, dt=F32):
            return ctx.enter_context(nc.sbuf_tensor(name, shape, dt))

        def sem(name):
            return ctx.enter_context(nc.semaphore(name))

        W0 = sb("W0", [P, KT, 3 * C])
        WP = sb("WP", [P, 4, C])
        W1 = sb("W1", [P, KT, NH, 3 * D])
        WO = sb("WO", [P, NH, C])
        CST = sb("CST", [P, 2 * P + 4])
        ident, same8 = CST[:, 0:P], CST[:, P:2 * P]
        HALVES = CST[:, 2 * P:2 * P + 2]
        QSC = CST[:, 2 * P + 3:2 * P + 4]
        EPSV = CST[:, 2 * P + 2:2 * P + 3]
        SMALL = 204
        SM = sb("SM", [P, SMALL])
        X = sb("X", [P, KT, L])
        XN = sb("XN", [P, KT, L])
        ARENA = 31098
        arena = sb("arena", [P, ARENA])
        PS = ctx.enter_context(nc.psum_tensor("PS", [P, 8, CH], F32))

        class Region:
            def __init__(self, tensor, size):
                self.t, self.size, self.at = tensor, size, 0

            def take(self, n):
                self.at += n
                assert self.at <= self.size, (self.at, self.size)
                return self.t[:, self.at - n:self.at]

        small = Region(SM, SMALL)
        STATS = small.take(KT * 8 * 6).rearrange("p (k c s) -> p k c s", k=KT, c=8)
        MV = small.take(2 * KT)
        GM = small.take(2 * KT)
        DEV = small.take(KT)
        SQ = small.take(KT)
        VAR = small.take(KT)
        STD = small.take(KT)
        RSTD = small.take(KT)
        NBIAS = small.take(KT)
        KSUM = small.take(2)
        BIAS = small.take(KT)
        LB = small.take(1)
        MX = small.take(12)
        SU = small.take(12)
        RC = small.take(12)
        NM = small.take(2)
        DNQ = small.take(4)
        RNQ = small.take(4)
        MX8 = small.take(8 * NH)

        l0 = Region(arena, ARENA)
        RAW = [l0.take(PL * PAD) for _ in range(3)]
        AGG = [RAW[1][:, 0:L], l0.take(L), l0.take(L)]
        IN = [l0.take(2 * PAD) for _ in range(3)]
        OUTG = [l0.take(2 * 256) for _ in range(3)]
        TW = [l0.take(2 * CH) for _ in range(2)]
        DW = [l0.take(8 * TAPS) for _ in range(2)]
        KTS = [l0.take(2 * P) for _ in range(2)]
        VTS = [l0.take(2 * (P + 1)) for _ in range(2)]
        WN, WD = [l0.take(P) for _ in range(2)], [l0.take(P) for _ in range(2)]
        DN = [l0.take(CH) for _ in range(2)]
        ADD0 = [AGG[1][:, k * CH:(k + 1) * CH] for k in range(2)]

        l1 = Region(arena, ARENA)
        KVB = l1.take(NBLK * KVW)
        kvb = KVB.rearrange("p (m n) -> p m n", m=NBLK)
        QS = l1.take(L)
        OT = l1.take(2 * L)
        VN = [l1.take(8 * D1) for _ in range(2)]
        QBD = l1.take(8 * P)
        PR = [l1.take(TOPK * D) for _ in range(2)]
        PT = [l1.take(TOPK * D) for _ in range(2)]
        GK = [l1.take(TOPK * D) for _ in range(4)]
        GV = [l1.take(TOPK // 2 * D1) for _ in range(4)]
        SG = [l1.take(8 * D) for _ in range(3)]
        ON = [l1.take(4 * D) for _ in range(2)]
        KVT = l1.take(D1)
        ADD1 = SG
        XBM = PR[0][:, 0:KT * NBLK].rearrange("p (k n) -> p k n", k=KT)
        QB, KB, SC = PT[0][:, 0:4 * NBLK], PT[1][:, 0:4 * NBLK], PR[1][:, 0:4 * NBLK]
        IUF = l1.take(8 * NH)
        IDX = sb("IDX", [D, 8 * NH], I32)
        IU = IUF[0:D, :].bitcast(U32)
        IDXR = l1.take(2 * 8 * NBLK)[0:1, :].bitcast(I32)

        def chunk_of(tile, c):
            f = 2 * c
            oy, ox = f // 8, (f % 4) // 2
            return tile.rearrange("p (f r c) -> p f r c", f=PL, r=PW)[:, f:f + 2, oy:oy + R, ox:ox + R]

        def raw_half(j, h):
            start = h * P + (PL * PAD - 36 * P if h >= 18 else 0)
            return RAW[j][:, start:start + P]

        def agg_half(j, h):
            return AGG[j][:, h * P:(h + 1) * P]

        def planes(ap):
            return ap.rearrange("p (f r c) -> p f r c", f=2, r=R)

        def natural(tile, fy):
            return tile.rearrange("p (r fy c fx) -> p fy fx r c", fy=4, c=R, fx=4)[:, fy]

        def x_planes(kt, c):
            f = 2 * c
            return natural(X[:, kt, :], f // 4)[:, f % 4:f % 4 + 2]

        s_w = sem("weights_loaded")
        s_wo = sem("wo_folded")
        s_bias = sem("bias_summed")
        s_ld = sem("x_loaded")
        s_st = sem("x_stored")
        s_mv = sem("channel_stats")
        s_gm = sem("group_sums")
        s_var = sem("group_variance")
        s_std = sem("group_std")
        s_rstd = sem("group_rstd")
        s_xna = sem("xn_by_act")
        s_xnd = sem("xn_by_dve")
        s_it = [sem("item_for_act"), sem("item_for_dve")]
        s_free = [sem("bank_freed_by_act"), sem("bank_freed_by_dve")]
        s_zero = sem("zeros_set")
        s_taps = [sem(f"taps_loaded{i}") for i in range(2)]
        s_tw = sem("toeplitz_built")
        s_in = [sem(f"conv_in{i}") for i in range(3)]
        s_og = [sem(f"conv_out{i}") for i in range(3)]
        s_kv = sem("kv_summed")
        s_w2 = sem("kv_weights")
        s_qr = sem("q_relu")
        s_xp = sem("x_added_by_pool")
        s_xbm = sem("block_sums")
        s_qkb = sem("block_qk")
        s_qkc = sem("block_qk_copied")
        s_sc = sem("block_scores")
        s_idx = sem("block_indices")
        s_ir = [sem(f"indices_in_row{i}") for i in range(2)]
        s_zero1 = sem("zeros_set_layer1")
        s_qp = sem("qkv_tokens")
        s_sub = sem("max_subtracted")
        s_raw = sem("qkv_copied")
        s_exp = sem("features_exp")
        s_rc = sem("feature_sums")
        s_nrm = sem("features_normalised")
        s_tb = sem("qk_turned")
        s_tbe = sem("qk_stored")
        s_vd = [sem(f"v_spread{i}") for i in range(2)]
        s_kvt = sem("kv_total")
        s_qbd = sem("q_block_diagonal")
        s_s = sem("scores")
        s_nm = sem("scores_max")
        s_lin = sem("linear_scores_copied")
        s_gk = sem("k_gathered_by_pool")
        s_gka = sem("k_gathered_by_act")
        s_gva = sem("v_gathered_by_act")
        s_gvd = sem("v_gathered_by_dve")
        s_p = sem("scores_exp")
        s_t = sem("probs_turned")
        s_pt = sem("probs_stored")
        s_o = sem("attended")
        s_on = sem("normalised")
        s_ont = sem("outputs_turned")
        s_one = sem("outputs_stored")
        s_settled = sem("settled")
        s_dve = sem("dve_order")
        s_dveb = sem("dve_order_tokens")
        s_dvec = sem("dve_order_attention")

        block = ctx.enter_context(nc.Block())

        def wait_emptied(eng, b, i):
            for e in range(2):
                eng.wait_ge(s_free[e], b * IT + 2 + count(i, e))

        def wait_filled(eng, b, i):
            eng.wait_ge(s_it[i % 2], b * IT + count(i, i % 2))

        LAST = (NBLK - 1) * KVW

        def settle(eng):
            eng.sem_inc(s_settled, 1)

        @block.sync
        def _(sp):
            for dst, src in ((W0[:], w0), (WP[:], wp), (W1[:], w1), (WO[0:D], wo), (CST[:], consts),
                             (arena[0:D, 0:P], lw), (LB[0:D, :], lb)):
                sp.dma_start(dst, src).then_inc(s_w, 16)
            sp.sem_inc(s_st, 16)
            for s in s_og:
                sp.sem_inc(s, 32)
            with sp.Fori(0, n_batch) as b:
                sp.wait_ge(s_st, b * 32 + 16)
                for kt in range(KT):
                    sp.dma_start(X[:, kt, :], x[bass.ds(b, 1), kt].rearrange("o p n -> (o p) n")).then_inc(s_ld, 16)

                def load_taps(t):
                    if t >= 2:
                        sp.wait_ge(s_tw, b * PAIRS + 4 * (t - 1))
                    g, j, hf = t // 6, PARTS[t % 6 // 2], t % 2
                    sp.dma_start(DW[t % 2], taps[j * 2 + g, hf]).then_inc(s_taps[t % 2], 16)

                def load_pair(n):
                    g, j, pr = n // 24, PARTS[n % 24 // 8], n % 8
                    if n % 4 == 0 and 1 <= n // 4 <= 10:
                        load_taps(n // 4 + 1)
                    if n >= 3:
                        wait_filled(sp, b, conv_item(n - 3))
                    if pr == 0:
                        settle(sp)
                        wait_emptied(sp, b, g * HALF_ITEMS + I_QKV + 8 * j + 7)
                    for a in range(2):
                        ch = 8 * (2 * pr + a)
                        sp.dma_start(IN[n % 3][:, a * PAD:(a + 1) * PAD],
                                     RAW[j][ch:ch + 8, :].rearrange("p (f n) -> p f n", f=PL)
                                     ).then_inc(s_in[n % 3], 16)

                def store_pair(n):
                    j, pr = PARTS[n % 24 // 8], n % 8
                    i = conv_item(n)
                    if n == 24:
                        sp.wait_ge(s_xp, b * XADDS + 8)
                        settle(sp)
                    sp.wait_ge(s_free[i % 2], b * IT + 2 + count(i, i % 2))
                    for a in range(2):
                        ch = 8 * (2 * pr + a)
                        sp.dma_start(AGG[j][ch:ch + 8, :].rearrange("p (f n) -> p f n", f=PL),
                                     OUTG[n % 3][:, a * 256:(a + 1) * 256]).then_inc(s_og[n % 3], 16)

                load_taps(0)
                load_taps(1)
                for g in range(2):
                    for k in range(24 + 2):
                        if k < 24:
                            load_pair(24 * g + k)
                        if k >= 2:
                            store_pair(24 * g + k - 2)
                sp.wait_ge(s_idx, b + 1)
                sp.wait_ge(s_zero1, b + 1)
                for hp in range(2):
                    if hp == 1:
                        sp.wait_ge(s_one, b * 64 + 32)
                    for hl in range(2):
                        h = 2 * hp + hl
                        sp.dma_start(IDXR[:, hl * 8 * NBLK:(hl + 1) * 8 * NBLK].rearrange("o (n k) -> o n k", k=8),
                                     IDX[:, 8 * h:8 * h + 8]).then_inc(s_ir[hl], 16)
                    with sp.Fori(0, 2) as hl:
                        hd = b * NH + 2 * hp + hl
                        for gr in range(4):
                            sp.wait_ge(s_raw, hd * TP + 4 * (gr + 1))
                            v = VN[gr % 2].rearrange("p (t n) -> p t n", t=8)[:, :, 0:D]
                            blocks = kvb.rearrange("p (t u) n -> p t u n", u=2)[:, 8 * gr:8 * gr + 8]
                            for u in range(2):
                                for half in range(2):
                                    sp.dma_start(blocks[D * half:D * (half + 1), :, u, D:2 * D],
                                                 v[D * u:D * (u + 1)]).then_inc(s_vd[gr % 2], 16)
                sp.wait_ge(s_xp, (b + 1) * XADDS)
                settle(sp)
                sp.wait_ge(s_free[1], b * IT + 2 + count(ITEMS - 1, 1))
                for kt in range(KT):
                    sp.dma_start(out[bass.ds(b, 1), kt].rearrange("o p n -> (o p) n"), X[:, kt, :]).then_inc(s_st, 16)
            sp.wait_ge(s_st, 32 * n_batch + 16)

        @block.gpsimd
        def _(pool):
            pool.wait_ge(s_bias, 2)
            pool_regs = [pool.alloc_register(f"k_offset{j}") for j in range(7)]
            with pool.Fori(0, n_batch) as b:
                pool.wait_ge(s_ld, (b + 1) * 32)
                settle(pool)
                for j in range(3):
                    pool.memset(RAW[j], 0.0).then_inc(s_zero, 1)
                for s in range(2):
                    pool.memset(VTS[s].rearrange("p (u n) -> p u n", u=2)[:, :, P:P + 1], 1.0).then_inc(s_zero, 1)

                def toeplitz(n):
                    t = n // 4
                    if n % 4 == 0:
                        pool.wait_ge(s_taps[t % 2], b * 96 + 16 * (t // 2 + 1))
                    if n >= 2:
                        wait_filled(pool, b, conv_item(n - 2))
                    dw = DW[t % 2].rearrange("p (h n) -> p h n", h=8)
                    for a in range(2):
                        hh = 2 * (n % 4) + a
                        o = TW[n % 2][:, a * CH:(a + 1) * CH].rearrange("p (k c q) -> p k c q", k=4, c=8)
                        tap = dw[:, hh, 0:64].rearrange("p (k q) -> p k q", k=4)
                        tap = tap.unsqueeze(2).broadcast_to([P, 4, 8, 16])
                        mix = dw[:, hh, 64:72].unsqueeze(1).unsqueeze(3).broadcast_to([P, 4, 8, 16])
                        last = pool.tensor_tensor(o, tap, mix, ALU.mult)
                    last.then_inc(s_tw, 1)

                def add_to_x(n, i, buf, target):
                    pool.wait_ge(s_free[0], b * IT + 2 + count(i, 0))
                    pool.tensor_tensor(target, target, buf, ALU.add).then_inc(s_xp, 1)

                for g in range(2):
                    for n in range(24 * g, 24 * g + 24):
                        toeplitz(n)
                    for k in range(3):
                        pool.wait_ge(s_in[k], b * 512 + 256 * (g + 1))
                    settle(pool)
                    for c in range(NCH):
                        pool.tensor_scalar(chunk_of(RAW[0], c), chunk_of(RAW[0], c), 0.0, None,
                                           ALU.max).then_inc(s_qr, 1)
                    for c in range(NCH):
                        add_to_x(8 * g + c, g * HALF_ITEMS + proj_item(c), planes(ADD0[c % 2]), x_planes(0, c))
                    if g == 0:
                        wait_filled(pool, b, HALF_ITEMS - 1)
                        settle(pool)
                        pool.memset(RAW[1], 0.0).then_inc(s_zero, 1)
                wait_filled(pool, b, L0_ITEMS - 1)
                settle(pool)
                pool.memset(kvb[:, :, 2 * D:KVW], 1.0)
                pool.memset(KVT, 0.0)
                for s in range(2):
                    last = pool.memset(VN[s].rearrange("p (t n) -> p t n", t=8)[:, :, D:D1], 1.0)
                last.then_inc(s_zero1, 1)
                for hp in range(2):
                    with pool.Fori(0, 2) as hl:
                        hd = b * NH + 2 * hp + hl
                        for p in range(TP):
                            sg = SG[p % 3].rearrange("p (u s d) -> p u s d", u=2, s=4)
                            feat = sg[:, :, 1:4:2, :]
                            rc = RC[:, 4 * (p % 3):4 * (p % 3) + 4].rearrange("p (u s) -> p u s", u=2)
                            pool.wait_ge(s_rc, hd * TP + p + 1)
                            pool.tensor_tensor(feat, feat, rc.unsqueeze(3).broadcast_to([P, 2, 2, D]),
                                               ALU.mult).then_inc(s_nrm, 1)
                        pool.wait_ge(s_tbe, (hd + 1) * TP)
                        settle(pool)

                        pool.wait_ge(s_ir[0], (b * 2 + hp + 1) * 16)
                        pool.wait_ge(s_ir[1], (b * 2 + hp + 1) * 16)
                        settle(pool)

                        def spread_q(start, u8):
                            src = QS[:, bass.ds(start + u8 * D, 2 * D)].rearrange("p (n c) -> p n c", n=2)
                            pool.tensor_tensor(QBD[:, u8 * P:(u8 + 2) * P].rearrange("p (n h c) -> p n h c", n=2, h=2),
                                               src.unsqueeze(2).broadcast_to([P, 2, 2, D]),
                                               HALVES.unsqueeze(1).unsqueeze(3).broadcast_to([P, 2, 2, D]),
                                               ALU.mult).then_inc(s_qbd, 2)

                        def eight(nb, row, start, first):
                            for u8 in range(8):
                                if u8 % 2 == 0:
                                    if not first:
                                        pool.wait_ge(s_o, nb + (u8 - 6))
                                        settle(pool)
                                    spread_q(start, u8)
                                pool.load(pool_regs, IDXR[:, bass.ds(row + 8 * u8, 7)])
                                off = [pool.snap(r, min_val=0, max_val=LAST) for r in pool_regs]
                                if not (first and u8 < 4):
                                    pool.wait_ge(s_s, nb + (u8 - 3))
                                    settle(pool)
                                for j in POOL_KEYS:
                                    last = pool.tensor_copy(GK[u8 % 4][:, j * D:(j + 1) * D],
                                                            KVB[:, bass.ds(off[j // 2 + 4 * (j % 2)], D)])
                                last.then_inc(s_gk, 1)

                        eight(pool.snap(hd * NBLK), pool.snap(hl * (8 * NBLK)), 0, True)
                        with pool.Fori(1, 8) as qq:
                            eight(pool.snap(hd * NBLK + 8 * qq), pool.snap(hl * (8 * NBLK) + 64 * qq),
                                  pool.snap(qq * (8 * D)), False)
                    for k in range(8):
                        i = 2 * k
                        add_to_x(16 + 8 * hp + k, L0_ITEMS + D_ITEMS * hp + i, ADD1[k % 2],
                                 X[:, i // 8, (i % 8) * CH:(i % 8 + 1) * CH])

        @block.tensor
        def _(pe):
            pe.wait_ge(s_w, 16 * 7)
            for h in range(NH):
                last = nc.tensor.matmul(PS[:, h // 2, (h % 2) * C:(h % 2 + 1) * C], lhsT=arena[0:D, 0:P],
                                        rhs=WO[0:D, h, :], start=True, stop=True)
            last.then_inc(s_wo, 1)
            for ot in range(KT):
                for h in range(NH):
                    last = nc.tensor.matmul(PS[:, 2 + ot, 0:1], lhsT=WO[0:D, h, ot * P:(ot + 1) * P],
                                            rhs=LB[0:D, :], start=(h == 0), stop=(h == NH - 1))
            last.then_inc(s_wo, 1)
            pe.wait_ge(s_bias, 2)
            with pe.Fori(0, n_batch) as b:
                def bank(i):
                    return PS[:, i % 4, :]

                def claim(i):
                    pe.wait_ge(s_free[i % 2], b * IT + i // 2 + 1)

                def hand(i, ins):
                    ins.then_inc(s_it[i % 2], 1)

                def group_sums(layer):
                    for k in range(2):
                        pe.wait_ge(s_mv, b * 4 + 2 * layer + 1 + k)
                        nc.tensor.matmul(PS[:, 6, 8 * k:8 * k + (4, 2)[k]], lhsT=same8, rhs=(MV, SQ)[k],
                                         start=True, stop=True).then_inc(s_gm, 1)

                group_sums(0)
                pe.wait_ge(s_xna, b * 8 + 4)
                pe.wait_ge(s_xnd, b * 8 + 4)
                for g in range(2):
                    base = g * HALF_ITEMS

                    def conv(i0, n0):
                        for pr in range(8):
                            i, n = i0 + pr, n0 + pr
                            claim(i)
                            pe.wait_ge(s_tw, b * PAIRS + n + 1)
                            pe.wait_ge(s_in[n % 3], b * 512 + 32 * (n // 3 + 1))
                            for a in range(2):
                                src = IN[n % 3][:, a * PAD:(a + 1) * PAD].rearrange("p (r c) -> p r c", r=PW)
                                for k in range(4):
                                    last = nc.tensor.matmul(
                                        bank(i)[:, a * 256:(a + 1) * 256],
                                        lhsT=TW[n % 2][:, a * CH + k * P:a * CH + (k + 1) * P],
                                        rhs=src[:, k // 2:k // 2 + R, k % 2:k % 2 + R],
                                        start=(k == 0), stop=(k == 3))
                            hand(i, last)

                    def kv_sums(src, half, item, then):
                        n_items = SUM_ITEMS[src]

                        def add_up(t):
                            i = item(t)
                            pe.wait_ge(s_free[i % 2], b * IT + 2 + count(i, i % 2))
                            for u in range(2):
                                last = nc.tensor.matmul(PS[:, 4 + src, 0:P + 1], lhsT=KTS[t % 2][:, u * P:(u + 1) * P],
                                                        rhs=VTS[t % 2][:, u * (P + 1):(u + 1) * (P + 1)],
                                                        start=(t == 0 and u == 0), stop=(t == n_items - 1 and u == 1))
                            if t == n_items - 1:
                                last.then_inc(s_kv, 1)
                        for t in range(n_items):
                            i = item(t)
                            claim(i)
                            for u in range(2):
                                nc.tensor.transpose(bank(i)[:, u * P:(u + 1) * P], half(1, 2 * t + u), ident)
                                last = nc.tensor.transpose(bank(i)[:, (2 + u) * P:(3 + u) * P],
                                                           half(2, 2 * t + u), ident)
                            hand(i, last)
                            if t >= 1:
                                add_up(t - 1)
                            if t % 2:
                                then(t // 2)
                        add_up(n_items - 1)

                    def attend(src, c):
                        q = chunk_of(RAW[0], c) if src == 0 else AGG[0][:, c * CH:(c + 1) * CH]
                        for i, w in ((base + att_item(src, c), WD[src]), (base + att_item(src, c) + 1, WN[src])):
                            claim(i)
                            hand(i, nc.tensor.matmul(bank(i), lhsT=w, rhs=q, start=True, stop=True))

                    def attend_raw(c):
                        pe.wait_ge(s_qr, b * 16 + 8 * g + c + 1)
                        attend(0, c)

                    def wait_stored(n):
                        for k in range(3):
                            pe.wait_ge(s_og[k], b * 512 + 32 * ((n - k) // 3 + 2))

                    for j in range(3):
                        for c in range(NCH):
                            i = base + I_QKV + 8 * j + c
                            claim(i)
                            for kt in range(KT):
                                last = nc.tensor.matmul(bank(i), lhsT=W0[:, kt, (2 * j + g) * P:(2 * j + g + 1) * P],
                                                        rhs=XN[:, kt, c * CH:(c + 1) * CH],
                                                        start=(kt == 0), stop=(kt == KT - 1))
                            hand(i, last)
                    conv(base + I_CK, 24 * g)
                    conv(base + I_CV, 24 * g + 8)
                    wait_emptied(pe, b, base + I_QKV + 23)
                    kv_sums(0, raw_half, lambda t: base + I_SUM0 + t, lambda c: None)
                    conv(base + I_CQ, 24 * g + 16)
                    wait_stored(24 * g + 15)
                    pe.wait_ge(s_w2, b * 4 + 2 * g + 1)
                    kv_sums(1, agg_half, lambda t: base + sum1_item(t), attend_raw)
                    pe.wait_ge(s_w2, b * 4 + 2 * g + 2)
                    wait_stored(24 * g + 23)
                    for c in range(NCH + 2):
                        if c < NCH:
                            attend(1, c)
                        if c >= 2:
                            i = base + att_item(1, c - 2) + 1
                            pe.wait_ge(s_free[1], b * IT + 2 + count(i, 1))
                            for ot in range(KT):
                                i = base + proj_item(c - 2) + ot
                                claim(i)
                                nc.tensor.matmul(bank(i), lhsT=WP[:, g, ot * P:(ot + 1) * P],
                                                 rhs=chunk_of(RAW[0], c - 2), start=True, stop=False)
                                hand(i, nc.tensor.matmul(bank(i), lhsT=WP[:, 2 + g, ot * P:(ot + 1) * P],
                                                         rhs=AGG[0][:, (c - 2) * CH:(c - 1) * CH],
                                                         start=False, stop=True))

                group_sums(1)
                pe.wait_ge(s_xbm, b + 1)
                for h in range(NH):
                    for part in range(2):
                        for kt in range(KT):
                            last = nc.tensor.matmul(PS[0:D, 5 + part, h * NBLK:(h + 1) * NBLK],
                                                    lhsT=W1[:, kt, h, part * D:(part + 1) * D], rhs=XBM[:, kt, :],
                                                    start=(kt == 0), stop=(kt == KT - 1))
                last.then_inc(s_qkb, 1)
                pe.wait_ge(s_qkc, b + 1)
                settle(pe)
                for h in range(NH):
                    cols = slice(h * NBLK, (h + 1) * NBLK)
                    last = nc.tensor.matmul(PS[0:D, 7, cols], lhsT=QB[0:D, cols], rhs=KB[0:D, cols],
                                            start=True, stop=True)
                last.then_inc(s_sc, 1)
                pe.wait_ge(s_sc, b + 1)
                pe.wait_ge(s_zero1, b + 1)
                pe.wait_ge(s_idx, b + 1)
                for hp in range(2):
                    wait_emptied(pe, b, L0_ITEMS + D_ITEMS * hp - 1)
                    settle(pe)
                    with pe.Fori(0, 2) as hl:
                        hd = b * NH + 2 * hp + hl

                        def turn(p):
                            pe.wait_ge(s_nrm, hd * TP + p + 1)
                            if p >= 2:
                                pe.wait_ge(s_tbe, hd * TP + p - 1)
                            sg = SG[p % 3]
                            vn = VN[p // 4 % 2]
                            for u in range(2):
                                k_ck = sg[:, (4 * u + 2) * D:(4 * u + 4) * D]
                                nc.tensor.transpose(PS[:, 2 + p % 2, u * P:(u + 1) * P],
                                                    sg[:, 4 * u * D:(4 * u + 2) * D], ident)
                                nc.tensor.transpose(PS[:, 2 + p % 2, (2 + u) * P:(3 + u) * P], k_ck, ident)
                            for u in range(2):
                                t = 2 * (p % 4) + u
                                last = nc.tensor.matmul(PS[:, 7, 0:D1], lhsT=sg[:, (4 * u + 2) * D:(4 * u + 4) * D],
                                                        rhs=vn[:, t * D1:(t + 1) * D1],
                                                        start=(p == 0 and u == 0), stop=(p == TP - 1 and u == 1))
                            last.then_inc(s_tb, 1)

                        for p in range(TP):
                            if p >= 2:
                                pe.wait_ge(s_raw, hd * TP + p - 1)
                            for u in range(2):
                                t = 2 * p + u
                                for kt in range(KT):
                                    last = nc.tensor.matmul(
                                        PS[:, p % 2, u * 3 * D:(u + 1) * 3 * D], lhsT=XN[:, kt, t * P:(t + 1) * P],
                                        rhs=W1[:, kt, bass.ds(2 * hp + hl, 1), :].rearrange("p o n -> p (o n)"),
                                        start=(kt == 0), stop=(kt == KT - 1))
                            last.then_inc(s_qp, 1)
                            if p >= 2:
                                turn(p - 2)
                        turn(TP - 2)
                        turn(TP - 1)
                        pe.wait_ge(s_tbe, (hd + 1) * TP)
                        for k in range(2):
                            pe.wait_ge(s_vd[k], (hd + 1) * 128)
                        pe.wait_ge(s_kvt, hd + 1)
                        def turn_probs(nb, u):
                            pe.wait_ge(s_p, nb + (u + 1))
                            pe.wait_ge(s_lin, nb + (u + 1))
                            u8 = u % 8
                            for j in range(3):
                                last = nc.tensor.transpose(PS[:, 2 + u8 % 2, j * P:(j + 1) * P],
                                                           PR[u8 % 2][:, j * P:(j + 1) * P], ident)
                            last.then_inc(s_t, 1)

                        def apply(nb, u):
                            pe.wait_ge(s_pt, nb + (u + 1))
                            pe.wait_ge(s_gva, nb + (u + 1))
                            pe.wait_ge(s_gvd, nb + (u + 1))
                            u8 = u % 8
                            o = PS[:, 4 + u8 // 4, (u8 % 4) * D1:(u8 % 4 + 1) * D1]
                            nc.tensor.matmul(o, lhsT=QBD[:, u8 * P:(u8 + 1) * P], rhs=KVT,
                                             start=True, stop=False)
                            for k in range(TOPK // 2):
                                last = nc.tensor.matmul(o, lhsT=PT[u8 % 2][:, k * P:(k + 1) * P],
                                                        rhs=GV[u8 % 4][:, k * D1:(k + 1) * D1],
                                                        start=False, stop=(k == TOPK // 2 - 1))
                            if u8 % 2:
                                last.then_inc(s_o, 2)

                        def turn_out(quad, s):
                            pe.wait_ge(s_on, hd * 16 + quad + 1)
                            if not isinstance(quad, int) or quad > 0:
                                pe.wait_ge(s_one, hd * 16 + quad)
                            for k in range(2):
                                last = nc.tensor.transpose(PS[:, 6, (2 * s + k) * P:(2 * s + k + 1) * P],
                                                           ON[s][:, k * P:(k + 1) * P], ident)
                            last.then_inc(s_ont, 1)

                        def step(nb, u8, first, quad):
                            if not (first and u8 < 2):
                                turn_probs(nb, u8 - 2)
                            if u8 % 2 == 0:
                                pe.wait_ge(s_qbd, nb + (u8 + 2))
                            pe.wait_ge(s_gk, nb + (u8 + 1))
                            pe.wait_ge(s_gka, nb + (u8 + 1))
                            nc.tensor.matmul(PS[:, u8 % 2, 0:TOPK * D], lhsT=QBD[:, u8 * P:(u8 + 1) * P],
                                             rhs=GK[u8 % 4], start=True, stop=True).then_inc(s_s, 1)
                            if not (first and u8 < 3):
                                apply(nb, u8 - 3)
                            if u8 % 4 == 0 and not first:
                                turn_out(quad - 2, u8 // 4)

                        nb = pe.snap(hd * NBLK)
                        for u8 in range(8):
                            step(nb, u8, True, u8 // 4)
                        with pe.Fori(1, 8) as qq:
                            nb = pe.snap(hd * NBLK + 8 * qq)
                            for u8 in range(8):
                                step(nb, u8, False, 2 * qq + u8 // 4)
                        nb = hd * NBLK + NBLK
                        turn_probs(nb, -2)
                        apply(nb, -3)
                        turn_probs(nb, -1)
                        turn_out(14, 0)
                        apply(nb, -2)
                        apply(nb, -1)
                        turn_out(15, 1)
                        pe.wait_ge(s_one, hd * 16 + 16)
                    for ot in range(KT):
                        for c in range(NCH):
                            i = L0_ITEMS + D_ITEMS * hp + NCH * ot + c
                            claim(i)
                            for hh in range(2):
                                last = nc.tensor.matmul(bank(i), lhsT=WO[:, 2 * hp + hh, ot * P:(ot + 1) * P],
                                                        rhs=OT[:, hh * L + c * CH:hh * L + (c + 1) * CH],
                                                        start=(hh == 0), stop=(hh == 1))
                            hand(i, last)

        def empty_half(eng, e, b, g, copy, relu, weights, attend, project):
            base = g * HALF_ITEMS

            def conv(i0, n0, op):
                for pr in range(8):
                    i, n = i0 + pr, n0 + pr
                    if i % 2 == e:
                        wait_filled(eng, b, i)
                        eng.wait_ge(s_og[n % 3], b * 512 + 32 * (n // 3 + 1))
                        op(OUTG[n % 3], PS[:, i % 4, :]).then_inc(s_free[e], 1)

            def turned(t, i):
                if i % 2 == e:
                    wait_filled(eng, b, i)
                    relu(KTS[t % 2], PS[:, i % 4, 0:2 * P])
                    copy(VTS[t % 2].rearrange("p (u n) -> p u n", u=2)[:, :, 0:P],
                         PS[:, i % 4, 2 * P:4 * P].rearrange("p (u n) -> p u n", u=2)).then_inc(s_free[e], 1)

            eng.wait_ge(s_zero, b * 6 + 5 + g)
            for j in range(3):
                for c in range(NCH):
                    i = base + I_QKV + 8 * j + c
                    if i % 2 == e:
                        wait_filled(eng, b, i)
                        copy(chunk_of(RAW[j], c), planes(PS[:, i % 4, :])).then_inc(s_free[e], 1)
            conv(base + I_CK, 24 * g, copy)
            conv(base + I_CV, 24 * g + 8, copy)
            for t in range(SUM_ITEMS[0]):
                turned(t, base + I_SUM0 + t)
            weights(0)
            conv(base + I_CQ, 24 * g + 16, relu)
            for t in range(SUM_ITEMS[1]):
                turned(t, base + sum1_item(t))
                if t % 2:
                    attend(0, t // 2)
            weights(1)
            for c in range(NCH + 2):
                if c < NCH:
                    attend(1, c)
                if c >= 2:
                    project(c - 2)

        def x_chunk(i):
            return X[:, i // NCH, (i % NCH) * CH:(i % NCH + 1) * CH]

        def norm_chunk(layer, kt, q):
            if layer == 0:
                return (XN[:, kt, :].rearrange("p (fy fx r c) -> p fy fx r c", fy=4, fx=4, r=R)[:, q],
                        natural(X[:, kt, :], q))
            cols = slice(q * L // 4, (q + 1) * L // 4)
            return XN[:, kt, cols], X[:, kt, cols]

        @block.scalar
        def _(act):
            def copy(o, i):
                return nc.scalar.activation(o, i, ACT.Copy)

            def relu(o, i):
                return nc.scalar.activation(o, i, ACT.Relu)

            act.wait_ge(s_wo, 1)
            for h in range(NH):
                last = copy(WO[D:P, h, :], PS[D:P, h // 2, (h % 2) * C:(h % 2 + 1) * C])
            last.then_inc(s_bias, 1)
            act.sem_inc(s_free[0], 2)
            act_k_regs = [act.alloc_register(f"k_offset{k}") for k in range(2)]
            act_regs = [act.alloc_register(f"v_offset{k}") for k in range(3)]
            with act.Fori(0, n_batch) as b:
                def normalise(layer):
                    act.wait_ge(s_var, b * 2 + layer + 1)
                    nc.scalar.activation(STD, VAR, ACT.Sqrt).then_inc(s_std, 1)
                    act.wait_ge(s_rstd, b * 2 + layer + 1)
                    for q in range(4):
                        dst, src = norm_chunk(layer, 1, q)
                        nc.scalar.activation(dst, src, ACT.Identity, bias=NBIAS[:, 1:2],
                                             scale=RSTD[:, 1:2]).then_inc(s_xna, 1)

                def chunk_for_pool(n, i, buf, bias):
                    wait_filled(act, b, i)
                    if n % 8 >= 2:
                        act.wait_ge(s_xp, b * XADDS + n - 1)
                    nc.scalar.activation(buf, PS[:, i % 4, :], ACT.Identity, bias=bias).then_inc(s_free[0], 1)

                normalise(0)
                for g in range(2):
                    def denominators(src, c):
                        i = g * HALF_ITEMS + att_item(src, c)
                        wait_filled(act, b, i)
                        k = 8 * src + c - 2
                        if k >= 0:
                            used = g * HALF_ITEMS + att_item(k // 8, k % 8) + 1
                            act.wait_ge(s_free[1], b * IT + 2 + count(used, 1))
                        nc.scalar.activation(DN[c % 2], PS[:, i % 4, :], ACT.Copy, bias=ATT_EPS).then_inc(s_free[0], 1)

                    def project(c):
                        chunk_for_pool(8 * g + c, g * HALF_ITEMS + proj_item(c), ADD0[c % 2], 0.0)

                    empty_half(act, 0, b, g, copy, relu, lambda src: None, denominators, project)

                normalise(1)
                act.wait_ge(s_qkb, b + 1)
                copy(QB[0:D, :], PS[0:D, 5, 0:4 * NBLK])
                copy(KB[0:D, :], PS[0:D, 6, 0:4 * NBLK]).then_inc(s_qkc, 1)
                act.wait_ge(s_zero1, b + 1)
                for hp in range(2):
                    act.wait_ge(s_xp, b * XADDS + 16 + 8 * hp)
                    settle(act)
                    with act.Fori(0, 2) as hl:
                        hd = b * NH + 2 * hp + hl

                        def store_turned(p):
                            act.wait_ge(s_tb, hd * TP + p + 1)
                            copy(kvb[:, 4 * p:4 * p + 4, 0:D],
                                 PS[:, 2 + p % 2, 2 * P:4 * P].rearrange("p (m n) -> p m n", m=4))
                            nc.scalar.activation(QS[:, p * 2 * P:(p + 1) * 2 * P], PS[:, 2 + p % 2, 0:2 * P], ACT.Copy,
                                                 scale=QSC).then_inc(s_tbe, 1)

                        for p in range(TP):
                            act.wait_ge(s_qp, hd * TP + p + 1)
                            if p % 4 == 0 and p >= 8:
                                act.wait_ge(s_vd[p // 4 % 2], hd * 128 + 64 * (p // 8))
                            sg = SG[p % 3].rearrange("p (u s d) -> p u s d", u=2, s=4)
                            ps = PS[:, p % 2, 0:6 * D].rearrange("p (u s d) -> p u s d", u=2, s=3)
                            vn = VN[p // 4 % 2].rearrange("p (t n) -> p t n", t=8)
                            copy(sg[:, :, 0:4:2, :], ps[:, :, 0:2, :])
                            copy(vn[:, 2 * (p % 4):2 * (p % 4) + 2, 0:D], ps[:, :, 2, :]).then_inc(s_raw, 1)
                            if p >= 3:
                                store_turned(p - 3)
                            act.wait_ge(s_sub, hd * TP + p + 1)
                            feat = sg[:, :, 1:4:2, :]
                            nc.scalar.activation(feat, feat, ACT.Exp).then_inc(s_exp, 1)
                        for p in range(TP - 3, TP):
                            store_turned(p)

                        def exp(nb, u):
                            act.wait_ge(s_nm, nb + (u + 1))
                            u8 = u % 8
                            nc.scalar.activation(PR[u8 % 2][0:D, :], PS[0:D, u8 % 2, 0:TOPK * D], ACT.Exp,
                                                 bias=NM[0:D, u8 % 2:u8 % 2 + 1]).then_inc(s_p, 1)

                        def store_probs(nb, u):
                            act.wait_ge(s_t, nb + (u + 1))
                            u8 = u % 8
                            copy(PT[u8 % 2], PS[:, 2 + u8 % 2, 0:TOPK * D]).then_inc(s_pt, 1)

                        def gather_v(row, u):
                            act.load(act_regs, IDXR[:, bass.ds(row + (8 * u + 4), 3)])
                            u8 = u % 8
                            for k in range(3):
                                off = act.snap(act_regs[k], min_val=0, max_val=LAST)
                                last = copy(GV[u8 % 4][D:P, k * D1:(k + 1) * D1], KVB[D:P, D:][:, bass.ds(off, D1)])
                            last.then_inc(s_gva, 1)

                        def gather_k(row, u8):
                            act.load(act_k_regs, IDXR[:, bass.ds(row + (8 * u8 + 4), 2)])
                            for k in range(2):
                                off = act.snap(act_k_regs[k], min_val=0, max_val=LAST)
                                last = copy(GK[u8 % 4][:, (2 * k + 1) * D:(2 * k + 2) * D], KVB[:, bass.ds(off, D)])
                            last.then_inc(s_gka, 1)

                        act.wait_ge(s_tbe, (hd + 1) * TP)
                        for k in range(2):
                            act.wait_ge(s_ir[k], (b * 2 + hp + 1) * 16)
                        settle(act)
                        nb, row = act.snap(hd * NBLK), act.snap(hl * (8 * NBLK))
                        for u8 in range(8):
                            gather_k(row, u8)
                            if u8 >= 2:
                                exp(nb, u8 - 2)
                                gather_v(row, u8 - 2)
                            if u8 >= 3:
                                store_probs(nb, u8 - 3)
                        with act.Fori(1, 8) as qq:
                            nb, row = act.snap(hd * NBLK + 8 * qq), act.snap(hl * (8 * NBLK) + 64 * qq)
                            for u8 in range(8):
                                gather_k(row, u8)
                                exp(nb, u8 - 2)
                                gather_v(row, u8 - 2)
                                store_probs(nb, u8 - 3)
                        nb, row = act.snap(hd * NBLK + NBLK), act.snap((hl + 1) * (8 * NBLK))
                        for u in (-2, -1):
                            exp(nb, u)
                            gather_v(row, u)
                            store_probs(nb, u - 1)
                        store_probs(nb, -1)
                    for k in range(8):
                        chunk_for_pool(16 + 8 * hp + k, L0_ITEMS + D_ITEMS * hp + 2 * k, ADD1[k % 2],
                                       BIAS[:, k // 4:k // 4 + 1] if hp else 0.0)

        @block.vector
        def _(dve):
            def copy(o, i):
                return nc.vector.tensor_copy(o, i)

            def relu(o, i):
                return nc.vector.tensor_scalar(o, i, 0.0, None, ALU.max)

            dve.wait_ge(s_wo, 2)
            nc.vector.tensor_copy(BIAS, PS[:, 2:4, 0]).then_inc(s_bias, 1)
            dve.sem_inc(s_free[1], 2)
            dve_regs = [dve.alloc_register(f"v_offset{k}") for k in range(3)]
            DVE_N = 2 * 6 + 4 + 4 * NCH + 3
            with dve.Fori(0, n_batch) as b:
                order = Order(dve, s_dve, b * DVE_N, DVE_N)

                def normalise(layer):
                    for kt in range(KT):
                        for c in range(8):
                            last = nc.vector.bn_stats(STATS[:, kt, c, :], X[:, kt, c * CH:(c + 1) * CH])
                    order.after(last)
                    settle(dve)
                    mv = MV.rearrange("p (k s) -> p k s", k=KT)
                    gm = GM.rearrange("p (k s) -> p k s", k=KT)
                    nc.vector.bn_aggr(mv[:, 0, :], STATS[:, 0])
                    nc.vector.bn_aggr(mv[:, 1, :], STATS[:, 1]).then_inc(s_mv, 1)
                    dve.wait_ge(s_gm, b * 4 + 2 * layer + 1)
                    order.after(nc.vector.tensor_scalar(GM, PS[:, 6, 0:2 * KT], 1.0 / 8, None, ALU.mult))
                    order.after(nc.vector.tensor_tensor(DEV, mv[:, :, 0], gm[:, :, 0], ALU.subtract))
                    nc.vector.tensor_tensor(SQ, DEV, DEV, ALU.mult).then_inc(s_mv, 1)
                    dve.wait_ge(s_gm, b * 4 + 2 * layer + 2)
                    order.after(nc.vector.scalar_tensor_tensor(out=VAR, in0=PS[:, 6, 8:8 + KT], scalar=1.0 / 8,
                                                               in1=gm[:, :, 1], op0=ALU.mult, op1=ALU.add))
                    nc.vector.tensor_scalar(VAR, VAR, GN_EPS, None, ALU.add).then_inc(s_var, 1)
                    dve.wait_ge(s_std, b * 2 + layer + 1)
                    order.after(nc.vector.reciprocal(RSTD, STD))
                    order.after(nc.vector.tensor_tensor(NBIAS, gm[:, :, 0], RSTD, ALU.mult))
                    nc.vector.tensor_scalar(NBIAS, NBIAS, -1.0, None, ALU.mult).then_inc(s_rstd, 1)
                    for q in range(4):
                        dst, src = norm_chunk(layer, 0, q)
                        nc.vector.tensor_scalar(dst, src, GM[:, 0:1], RSTD[:, 0:1], ALU.subtract,
                                                ALU.mult).then_inc(s_xnd, 1)

                dve.wait_ge(s_ld, (b + 1) * 32)
                normalise(0)
                for g in range(2):
                    def kv_weights(src):
                        dve.wait_ge(s_kv, b * 4 + 2 * g + src + 1)
                        order.after(nc.vector.tensor_copy(KSUM[:, src:src + 1], PS[:, 4 + src, P:P + 1]))
                        nc.vector.tensor_tensor(WN[src], PS[:, 4 + src, 0:P], same8, ALU.mult)
                        nc.vector.tensor_scalar(WD[src], same8, KSUM[:, src:src + 1], None,
                                                ALU.mult).then_inc(s_w2, 1)

                    def divide(src, c):
                        i = g * HALF_ITEMS + att_item(src, c)
                        dve.wait_ge(s_free[0], b * IT + 2 + count(i, 0))
                        order.after(nc.vector.reciprocal(DN[c % 2], DN[c % 2]))
                        wait_filled(dve, b, i + 1)
                        ps = PS[:, (i + 1) % 4, :]
                        if src == 0:
                            nc.vector.tensor_tensor(chunk_of(RAW[0], c), planes(ps), planes(DN[c % 2]),
                                                    ALU.mult).then_inc(s_free[1], 1)
                        else:
                            nc.vector.tensor_tensor(AGG[0][:, c * CH:(c + 1) * CH], ps, DN[c % 2],
                                                    ALU.mult).then_inc(s_free[1], 1)

                    def project(c):
                        i = g * HALF_ITEMS + proj_item(c) + 1
                        wait_filled(dve, b, i)
                        nc.vector.tensor_tensor(x_planes(1, c), planes(PS[:, i % 4, :]), x_planes(1, c),
                                                ALU.add).then_inc(s_free[1], 1)

                    empty_half(dve, 1, b, g, copy, relu, kv_weights, divide, project)

                dve.wait_ge(s_xp, b * XADDS + 16)
                dve.wait_ge(s_free[1], b * IT + 2 + count(L0_ITEMS - 1, 1))
                normalise(1)
                dve.wait_ge(s_xna, b * 8 + 8)
                dve.wait_ge(s_xnd, b * 8 + 8)
                for kt in range(KT):
                    ins = nc.vector.tensor_reduce(XBM[:, kt, :], XN[:, kt, :].rearrange("p (m t) -> p m t", m=NBLK),
                                                  AX.X, ALU.add)
                ins.then_inc(s_xbm, 1)
                dve.wait_ge(s_sc, b + 1)
                order.after(copy(SC[0:D, :], PS[0:D, 7, 0:4 * NBLK]))
                settle(dve)
                for h in range(NH):
                    last = nc.vector.max(MX8[0:D, 8 * h:8 * h + 8], SC[0:D, h * NBLK:(h + 1) * NBLK])
                order.after(last)
                settle(dve)
                for h in range(NH):
                    last = nc.vector.max_index(IU[:, 8 * h:8 * h + 8], MX8[0:D, 8 * h:8 * h + 8],
                                               SC[0:D, h * NBLK:(h + 1) * NBLK])
                order.after(last)
                idx, iu = IDX[:].rearrange("p (h k) -> p h k", h=NH), IU.rearrange("p (h k) -> p h k", h=NH)
                nc.vector.tensor_scalar(idx[:, :, 0:4], iu[:, :, 0:4], float(KVW), None, ALU.mult)
                nc.vector.tensor_scalar(idx[:, :, 4:8], iu[:, :, 3:7], float(KVW), None, ALU.mult).then_inc(s_idx, 1)
                for hp in range(2):
                    with dve.Fori(0, 2) as hl:
                        hd = b * NH + 2 * hp + hl
                        torder = Order(dve, s_dveb, hd * 2 * TP, 2 * TP)

                        def sums(p):
                            dve.wait_ge(s_exp, hd * TP + p + 1)
                            feat = SG[p % 3].rearrange("p (u s d) -> p u s d", u=2, s=4)[:, :, 1:4:2, :]
                            part = slice(4 * (p % 3), 4 * (p % 3) + 4)
                            torder.after(nc.vector.tensor_reduce(SU[:, part].rearrange("p (u s) -> p u s", u=2), feat,
                                                                 AX.X, ALU.add))
                            nc.vector.reciprocal(RC[:, part], SU[:, part]).then_inc(s_rc, 1)

                        for p in range(TP):
                            dve.wait_ge(s_raw, hd * TP + p + 1)
                            sg = SG[p % 3].rearrange("p (u s d) -> p u s d", u=2, s=4)
                            qk, feat = sg[:, :, 0:4:2, :], sg[:, :, 1:4:2, :]
                            mx = MX[:, 4 * (p % 3):4 * (p % 3) + 4].rearrange("p (u s) -> p u s", u=2)
                            torder.after(nc.vector.tensor_reduce(mx, qk, AX.X, ALU.max))
                            nc.vector.tensor_tensor(feat, qk, mx.unsqueeze(3).broadcast_to([P, 2, 2, D]),
                                                    ALU.subtract).then_inc(s_sub, 1)
                            if p >= 1:
                                sums(p - 1)
                        sums(TP - 1)
                        torder.close()
                        dve.wait_ge(s_tb, (hd + 1) * TP)
                        nc.vector.tensor_scalar(KVT[D:P, :], PS[D:P, 7, 0:D1], -1.0, None,
                                                ALU.mult).then_inc(s_kvt, 1)

                        def maxima(nb, u8):
                            dve.wait_ge(s_s, nb + (u8 + 1))
                            nc.vector.tensor_reduce(NM[0:D, u8 % 2:u8 % 2 + 1], PS[0:D, u8 % 2, 0:TOPK * D], AX.X,
                                                    ALU.max, negate=True).then_inc(s_nm, 1)
                            copy(PR[u8 % 2][D:P, :], PS[D:P, u8 % 2, 0:TOPK * D]).then_inc(s_lin, 1)

                        def normalise_out(quad, s):
                            o = PS[:, 4 + s, 0:4 * D1].rearrange("p (n c) -> p n c", n=4)
                            chain = hd * 32 + 2 * quad
                            dve.wait_ge(s_o, hd * NBLK + 4 * quad + 4)
                            nc.vector.tensor_scalar(DNQ.unsqueeze(2), o[:, :, D:D1], EPSV, None,
                                                    ALU.add).then_inc(s_dvec, 1)
                            dve.wait_ge(s_dvec, chain + 1)
                            nc.vector.reciprocal(RNQ, DNQ).then_inc(s_dvec, 1)
                            dve.wait_ge(s_dvec, chain + 2)
                            on = ON[s].rearrange("p (k c) -> p k c", k=2)
                            for u in range(2):
                                for lin in range(2):
                                    rows = slice(D * lin, D * (lin + 1))
                                    last = nc.vector.tensor_tensor(
                                        on[D * u:D * (u + 1), :, D * lin:D * (lin + 1)], o[rows, u:4:2, 0:D],
                                        RNQ[rows, u:4:2].unsqueeze(2).broadcast_to([D, 2, D]), ALU.mult)
                            last.then_inc(s_on, 1)

                        def store_out(quad, s):
                            dve.wait_ge(s_ont, hd * 16 + quad + 1)
                            copy(OT[:, bass.ds(hl * L + quad * 4 * D, 4 * D)],
                                 PS[:, 6, 2 * s * P:(2 * s + 2) * P]).then_inc(s_one, 1)

                        def gather_v(row, u8):
                            dve.load(dve_regs, IDXR[:, bass.ds(row + 8 * u8, 3)])
                            for k in range(3):
                                off = dve.snap(dve_regs[k], min_val=0, max_val=LAST)
                                last = copy(GV[u8 % 4][0:D, k * D1:(k + 1) * D1], KVB[0:D, D:][:, bass.ds(off, D1)])
                            last.then_inc(s_gvd, 1)

                        def step(nb, row, u8, first, quad):
                            maxima(nb, u8)
                            gather_v(row, u8)
                            if u8 % 4 == 1 and not (first and u8 <= 5):
                                store_out(quad - 2, u8 // 4)
                            if u8 % 4 == 3 and not (first and u8 == 3):
                                normalise_out(quad - 1, (u8 // 4 + 1) % 2)

                        nb, row = dve.snap(hd * NBLK), dve.snap(hl * (8 * NBLK))
                        for u8 in range(8):
                            step(nb, row, u8, True, u8 // 4)
                        with dve.Fori(1, 8) as qq:
                            nb, row = dve.snap(hd * NBLK + 8 * qq), dve.snap(hl * (8 * NBLK) + 64 * qq)
                            for u8 in range(8):
                                step(nb, row, u8, False, 2 * qq + u8 // 4)
                        store_out(14, 0)
                        normalise_out(15, 1)
                        store_out(15, 1)
                    for k in range(8):
                        i = 2 * k + 1
                        wait_filled(dve, b, L0_ITEMS + D_ITEMS * hp + i)
                        xc = x_chunk(i)
                        if hp == 0:
                            ins = nc.vector.tensor_tensor(xc, PS[:, i % 4, :], xc, ALU.add)
                        else:
                            ins = nc.vector.scalar_tensor_tensor(out=xc, in0=PS[:, i % 4, :],
                                                                 scalar=BIAS[:, i // NCH:i // NCH + 1], in1=xc,
                                                                 op0=ALU.add, op1=ALU.add)
                        ins.then_inc(s_free[1], 1)
                order.close()


def kernel(**inputs):
    import numpy as np
    import concourse.bacc as bacc
    from concourse.bass_utils import run_bass_kernel_spmd as run

    x = np.ascontiguousarray(inputs["x"])
    n_batch = x.shape[0]
    a = {"x": x.reshape(n_batch, KT, P, L)}
    perm = (24 * np.arange(32)[None, :, None] + 8 * np.arange(3)[:, None, None] + np.arange(8)).reshape(-1)
    w = np.asarray(inputs["L0_conv_w_qkv"])[perm, :, 0, 0]
    a["w0"] = w.T.reshape(KT, P, 3 * C).transpose(1, 0, 2)
    dw = np.asarray(inputs["L0_conv_w_dw"])[perm, 0]
    padded = np.pad(dw, ((0, 0), (3, 3), (3, 3)))
    plane = (np.arange(4) + 2) % 4
    t = 4 * np.arange(2)[None, :, None] + plane[:, None, None] - np.arange(4)[None, None, :] + 3
    tt = padded[:, t[:, :, :, None, None, None], t[None, None, None]]
    tt = tt.transpose(0, 1, 4, 2, 5, 3, 6).reshape(96, 8 * 16, 64)
    pw = np.asarray(inputs["L0_conv_w_pw"])[perm, :, 0, 0].reshape(96, 8, 8)
    pw = np.repeat(pw.transpose(0, 2, 1), 16, axis=1)
    a["taps"] = np.concatenate([tt, pw], axis=2).reshape(6, 2, 8, P, TAPS).transpose(0, 1, 3, 2, 4).reshape(
        6, 2, P, 8 * TAPS)
    a["wp"] = np.asarray(inputs["L0_conv_w_proj"])[:, :, 0, 0].T.reshape(4, P, C).transpose(1, 0, 2)
    w = np.asarray(inputs["L1_conv_qkv_w"]).reshape(3, NH, D, C)
    a["w1"] = w.transpose(3, 1, 0, 2).reshape(KT, P, NH, 3 * D).transpose(1, 0, 2, 3)
    a["wo"] = np.asarray(inputs["L1_conv_out_w"]).T.reshape(NH, D, C).transpose(1, 0, 2)
    a["lw"] = np.pad(np.asarray(inputs["L1_conv_proj_lw"]), ((0, 0), (D, 0)))
    a["lb"] = np.asarray(inputs["L1_conv_proj_lb"])[:, None]
    group = np.arange(P) // 8
    lower = np.arange(P)[:, None] >= D
    a["consts"] = np.concatenate([np.eye(P), group[:, None] == group[None, :], ~lower, lower, -LIN_EPS * lower,
                                  np.where(lower, 1.0, D ** -0.5)],
                                 axis=1).astype(np.float32)

    nc = bacc.Bacc("TRN2", target_bir_lowering=False, num_devices=1)
    arrays, args = {}, []
    for name, v in a.items():
        v = np.ascontiguousarray(v)
        arrays[f"in_{name}"] = v
        args.append(nc.dram_tensor(f"in_{name}", v.shape, mybir.dt.from_np(v.dtype), kind="ExternalInput").ap())
    out = nc.dram_tensor("out", (n_batch, KT, P, L), F32, kind="ExternalOutput").ap()
    build(nc, *args, out, n_batch)
    r = run(nc, [arrays], core_ids=[0])
    return r.results[0]["out"].reshape(n_batch, C, HH, WW)
```

```python
from contextlib import ExitStack

import concourse.bass as bass
from concourse import mybir

F32 = mybir.dt.float32
I32 = mybir.dt.int32
U32 = mybir.dt.uint32
ALU = mybir.AluOpType
ACT = mybir.ActivationFunctionType
AX = mybir.AxisListType

P = 128
C, HH, WW = 256, 64, 64
L = HH * WW
KT = C // P
PL, R = 16, 16
PW = R + 1
PAD = PW * PW
CH = 512
NCH = L // CH
NH, D = 4, 64
NBLK = L // D
TOPK = 6
D1 = D + 1
KVW = D + D1
GN_EPS, ATT_EPS, LIN_EPS = 1e-5, 1e-15, 1e-6

I_QKV, I_SUM0, I_CQ, I_CKV, I_SUM1, I_LAST, HALF_ITEMS = 0, 24, 42, 50, 82, 98, 130
L0_ITEMS = 2 * HALF_ITEMS
D_ITEMS = KT * NCH
ITEMS = L0_ITEMS + 2 * D_ITEMS
IT = ITEMS // 2
SUM_ITEMS = (18, 16)
PAIRS = 48
TAPS = 72
TP = 16
POOL_KEYS = (0, 2, 4, 5)
XADDS = 32


def conv_item(n):
    g, m = n // 24, n % 24 - 8
    return g * HALF_ITEMS + (I_CQ + m + 8 if m < 0 else I_CKV + m + 2 * max(0, (m - 2) // 2))


def att_item(src, c):
    return I_CKV + min(2 * c + 4, 16) + 2 * c if src == 0 else I_LAST + max(2 * c, 4 * c - 4)


def proj_item(c):
    return I_LAST + min(4 * c + 6, 2 * c + 16)


def count(i, e):
    return (i - e) // 2 + 1


class Order:

    def __init__(self, eng, sem, base, total):
        self.eng, self.sem, self.base, self.total, self.n = eng, sem, base, total, 0

    def after(self, ins):
        self.n += 1
        ins.then_inc(self.sem, 1)
        self.eng.wait_ge(self.sem, self.base + self.n)

    def close(self):
        assert self.n == self.total, (self.n, self.total)


def build(nc, x, w0, taps, wp, w1, wo, lw, lb, consts, out, n_batch):
    with ExitStack() as ctx:
        def sb(name, shape, dt=F32):
            return ctx.enter_context(nc.sbuf_tensor(name, shape, dt))

        def sem(name):
            return ctx.enter_context(nc.semaphore(name))

        W0 = sb("W0", [P, KT, 3 * C])
        WP = sb("WP", [P, 4, C])
        W1 = sb("W1", [P, KT, NH, 3 * D])
        WO = sb("WO", [P, NH, C])
        CST = sb("CST", [P, 2 * P + 4])
        ident, same8 = CST[:, 0:P], CST[:, P:2 * P]
        HALVES = CST[:, 2 * P:2 * P + 2]
        QSC = CST[:, 2 * P + 3:2 * P + 4]
        EPSV = CST[:, 2 * P + 2:2 * P + 3]
        SMALL = 204
        SM = sb("SM", [P, SMALL])
        BUF = [sb(f"BUF{k}", [P, KT, L]) for k in range(2)]
        ARENA = 31098
        arena = sb("arena", [P, ARENA])
        PS = ctx.enter_context(nc.psum_tensor("PS", [P, 8, CH], F32))

        class Region:
            def __init__(self, tensor, size):
                self.t, self.size, self.at = tensor, size, 0

            def take(self, n):
                self.at += n
                assert self.at <= self.size, (self.at, self.size)
                return self.t[:, self.at - n:self.at]

        small = Region(SM, SMALL)
        STATS = small.take(KT * 8 * 6).rearrange("p (k c s) -> p k c s", k=KT, c=8)
        MV = small.take(2 * KT)
        GM = small.take(2 * KT)
        DEV = small.take(KT)
        SQ = small.take(KT)
        VAR = small.take(KT)
        STD = small.take(KT)
        RSTD = small.take(KT)
        NBIAS = small.take(KT)
        KSUM = small.take(2)
        BIAS = small.take(KT)
        LB = small.take(1)
        MX = small.take(12)
        SU = small.take(12)
        RC = small.take(12)
        NM = small.take(2)
        DNQ = small.take(4)
        RNQ = small.take(4)
        MX8 = small.take(8 * NH)

        l0 = Region(arena, ARENA)
        RAW = [l0.take(PL * PAD) for _ in range(3)]
        AGG = [l0.take(L), l0.take(L), RAW[1][:, 0:L]]
        IN = [l0.take(2 * PAD) for _ in range(3)]
        OUTG = [l0.take(2 * 256) for _ in range(3)]
        TW = [l0.take(2 * CH) for _ in range(2)]
        DW = [l0.take(8 * TAPS) for _ in range(2)]
        KTS = [l0.take(2 * P) for _ in range(2)]
        VTS = [l0.take(2 * (P + 1)) for _ in range(2)]
        WN, WD = [l0.take(P) for _ in range(2)], [l0.take(P) for _ in range(2)]
        DN = [l0.take(CH) for _ in range(2)]
        ADD0 = [AGG[1][:, k * CH:(k + 1) * CH] for k in range(2)]

        l1 = Region(arena, ARENA)
        KVB = l1.take(NBLK * KVW)
        kvb = KVB.rearrange("p (m n) -> p m n", m=NBLK)
        QS = l1.take(L)
        OT = l1.take(2 * L)
        VN = [l1.take(8 * D1) for _ in range(2)]
        QBD = l1.take(8 * P)
        PR = [l1.take(TOPK * D) for _ in range(2)]
        PT = [l1.take(TOPK * D) for _ in range(2)]
        GK = [l1.take(TOPK * D) for _ in range(4)]
        GV = [l1.take(TOPK // 2 * D1) for _ in range(4)]
        SG = [l1.take(8 * D) for _ in range(3)]
        ON = [l1.take(4 * D) for _ in range(2)]
        KVT = l1.take(D1)
        ADD1 = SG
        XBM = PR[0][:, 0:KT * NBLK].rearrange("p (k n) -> p k n", k=KT)
        QB, KB, SC = PT[0][:, 0:4 * NBLK], PT[1][:, 0:4 * NBLK], PR[1][:, 0:4 * NBLK]
        IUF = l1.take(8 * NH)
        IDX = sb("IDX", [D, 8 * NH], I32)
        IU = IUF[0:D, :].bitcast(U32)
        IDXR = l1.take(2 * 8 * NBLK)[0:1, :].bitcast(I32)

        def chunk_of(tile, c):
            f = 2 * c
            oy, ox = f // 8, (f % 4) // 2
            return tile.rearrange("p (f r c) -> p f r c", f=PL, r=PW)[:, f:f + 2, oy:oy + R, ox:ox + R]

        def raw_half(j, h):
            start = h * P + (PL * PAD - 36 * P if h >= 18 else 0)
            return RAW[j][:, start:start + P]

        def agg_half(j, h):
            return AGG[j][:, h * P:(h + 1) * P]

        def planes(ap):
            return ap.rearrange("p (f r c) -> p f r c", f=2, r=R)

        def natural(tile, fy):
            return tile.rearrange("p (r fy c fx) -> p fy fx r c", fy=4, c=R, fx=4)[:, fy]

        def x_planes(X, kt, c):
            f = 2 * c
            return natural(X[:, kt, :], f // 4)[:, f % 4:f % 4 + 2]

        s_w = sem("weights_loaded")
        s_wo = sem("wo_folded")
        s_bias = sem("bias_summed")
        s_ld = sem("x_loaded")
        s_st = [[sem(f"x_stored{kt}_{q}") for q in range(4)] for kt in range(KT)]
        s_mv = sem("channel_stats")
        s_gm = sem("group_sums")
        s_var = sem("group_variance")
        s_std = sem("group_std")
        s_rstd = sem("group_rstd")
        s_xna = sem("xn_by_act")
        s_xnd = sem("xn_by_dve")
        s_it = [sem("item_for_act"), sem("item_for_dve")]
        s_free = [sem("bank_freed_by_act"), sem("bank_freed_by_dve")]
        s_zero = sem("zeros_set")
        s_taps = [sem(f"taps_loaded{i}") for i in range(2)]
        s_tw = sem("toeplitz_built")
        s_in = [sem(f"conv_in{i}") for i in range(3)]
        s_og = [sem(f"conv_out{i}") for i in range(3)]
        s_kv = sem("kv_summed")
        s_w2 = sem("kv_weights")
        s_qr = sem("q_relu")
        s_xp = sem("x_added_by_pool")
        s_xbm = sem("block_sums")
        s_qkb = sem("block_qk")
        s_qkc = sem("block_qk_copied")
        s_sc = sem("block_scores")
        s_idx = sem("block_indices")
        s_ir = [sem(f"indices_in_row{i}") for i in range(2)]
        s_zero1 = sem("zeros_set_layer1")
        s_qp = sem("qkv_tokens")
        s_sub = sem("max_subtracted")
        s_raw = sem("qkv_copied")
        s_exp = sem("features_exp")
        s_rc = sem("feature_sums")
        s_nrm = sem("features_normalised")
        s_tb = sem("qk_turned")
        s_tbe = sem("qk_stored")
        s_vd = [sem(f"v_spread{i}") for i in range(2)]
        s_kvt = sem("kv_total")
        s_qbd = sem("q_block_diagonal")
        s_s = sem("scores")
        s_nm = sem("scores_max")
        s_lin = sem("linear_scores_copied")
        s_gk = sem("k_gathered_by_pool")
        s_gka = sem("k_gathered_by_act")
        s_gva = sem("v_gathered_by_act")
        s_gvd = sem("v_gathered_by_dve")
        s_p = sem("scores_exp")
        s_t = sem("probs_turned")
        s_pt = sem("probs_stored")
        s_o = sem("attended")
        s_on = sem("normalised")
        s_ont = sem("outputs_turned")
        s_one = sem("outputs_stored")
        s_settled = sem("settled")
        s_dve = sem("dve_order")
        s_dveb = sem("dve_order_tokens")
        s_dvec = sem("dve_order_attention")

        block = ctx.enter_context(nc.Block())

        def wait_emptied(eng, b, i):
            for e in range(2):
                eng.wait_ge(s_free[e], b * IT + 2 + count(i, e))

        def wait_filled(eng, b, i):
            eng.wait_ge(s_it[i % 2], b * IT + count(i, i % 2))

        LAST = (NBLK - 1) * KVW

        def settle(eng):
            eng.sem_inc(s_settled, 1)

        @block.sync
        def _(sp):
            for dst, src in ((W0[:], w0), (WP[:], wp), (W1[:], w1), (WO[0:D], wo), (CST[:], consts),
                             (arena[0:D, 0:P], lw), (LB[0:D, :], lb)):
                sp.dma_start(dst, src).then_inc(s_w, 16)
            for kt in range(KT):
                for q in range(4):
                    sp.sem_inc(s_st[kt][q], 16)
            for s in s_og:
                sp.sem_inc(s, 32)
            for kt in range(KT):
                sp.dma_start(BUF[0][:, kt, :], x[0, kt]).then_inc(s_ld, 16)
            with sp.Fori(0, n_batch // 2) as pair:
                for half in range(2):
                    b = sp.snap(2 * pair + half)
                    X, XN = BUF[half], BUF[1 - half]

                    def load_taps(t):
                        if t >= 2:
                            sp.wait_ge(s_tw, b * PAIRS + 4 * (t - 1))
                        g, j, hf = t // 6, t % 6 // 2, t % 2
                        sp.dma_start(DW[t % 2], taps[j * 2 + g, hf]).then_inc(s_taps[t % 2], 16)

                    def load_pair(n):
                        g, j, pr = n // 24, n % 24 // 8, n % 8
                        if n % 4 == 0 and 1 <= n // 4 <= 10:
                            load_taps(n // 4 + 1)
                        if n >= 3:
                            wait_filled(sp, b, conv_item(n - 3))
                        if pr == 0:
                            settle(sp)
                            wait_emptied(sp, b, g * HALF_ITEMS + I_QKV + 8 * j + 7)
                        for a in range(2):
                            ch = 8 * (2 * pr + a)
                            sp.dma_start(IN[n % 3][:, a * PAD:(a + 1) * PAD],
                                         RAW[j][ch:ch + 8, :].rearrange("p (f n) -> p f n", f=PL)
                                         ).then_inc(s_in[n % 3], 16)

                    def store_pair(n):
                        j, pr = n % 24 // 8, n % 8
                        i = conv_item(n)
                        if n == 24:
                            sp.wait_ge(s_xp, b * XADDS + 8)
                            settle(sp)
                        sp.wait_ge(s_free[i % 2], b * IT + 2 + count(i, i % 2))
                        for a in range(2):
                            ch = 8 * (2 * pr + a)
                            sp.dma_start(AGG[j][ch:ch + 8, :].rearrange("p (f n) -> p f n", f=PL),
                                         OUTG[n % 3][:, a * 256:(a + 1) * 256]).then_inc(s_og[n % 3], 16)

                    load_taps(0)
                    load_taps(1)
                    for g in range(2):
                        for k in range(24 + 2):
                            if k < 24:
                                load_pair(24 * g + k)
                            if k >= 2:
                                store_pair(24 * g + k - 2)
                    sp.wait_ge(s_idx, b + 1)
                    sp.wait_ge(s_zero1, b + 1)
                    for hp in range(2):
                        if hp == 1:
                            sp.wait_ge(s_one, b * 64 + 32 + 1)
                        for hl in range(2):
                            h = 2 * hp + hl
                            sp.dma_start(IDXR[:, hl * 8 * NBLK:(hl + 1) * 8 * NBLK].rearrange("o (n k) -> o n k", k=8),
                                         IDX[:, 8 * h:8 * h + 8]).then_inc(s_ir[hl], 16)
                        with sp.Fori(0, 2) as hl:
                            hd = b * NH + 2 * hp + hl
                            for gr in range(4):
                                sp.wait_ge(s_raw, hd * TP + 4 * (gr + 1))
                                v = VN[gr % 2].rearrange("p (t n) -> p t n", t=8)[:, :, 0:D]
                                blocks = kvb.rearrange("p (t u) n -> p t u n", u=2)[:, 8 * gr:8 * gr + 8]
                                for u in range(2):
                                    for half in range(2):
                                        sp.dma_start(blocks[D * half:D * (half + 1), :, u, D:2 * D],
                                                     v[D * u:D * (u + 1)]).then_inc(s_vd[gr % 2], 16)
                    sp.wait_ge(s_tbe, (b + 1) * NH * TP)
                    settle(sp)
                    nxt = sp.snap((b + 1) % n_batch, min_val=0, max_val=n_batch - 1)
                    for kt in range(KT):
                        sp.dma_start(XN[:, kt, :], x[bass.ds(nxt, 1), kt].rearrange("o p n -> (o p) n")
                                     ).then_inc(s_ld, 16)
                    for kt in range(KT):
                        for q in range(4):
                            sp.wait_ge(s_xp, b * XADDS + 24 + 4 * kt + q + 1)
                            settle(sp)
                            sp.wait_ge(s_free[1], b * IT + 2 + count(ITEMS - D_ITEMS + 8 * kt + 2 * q + 1, 1))
                            cols = slice(q * L // 4, (q + 1) * L // 4)
                            sp.dma_start(out[bass.ds(b, 1), kt, :, cols].rearrange("o p n -> (o p) n"),
                                         X[:, kt, cols]).then_inc(s_st[kt][q], 16)
            for kt in range(KT):
                for q in range(4):
                    sp.wait_ge(s_st[kt][q], 16 * n_batch + 16)
            sp.wait_ge(s_ld, 32 * (n_batch + 1))

        @block.gpsimd
        def _(pool):
            pool.wait_ge(s_bias, 2)
            pool_regs = [pool.alloc_register(f"k_offset{j}") for j in range(7)]

            def clear_halo(j):
                tile = RAW[j].rearrange("p (oy y ox x r c) -> p oy y ox x r c", oy=2, y=2, ox=2, x=2, r=PW)
                by_oy = RAW[j].rearrange("p (oy f r c) -> p oy f r c", oy=2, f=8, r=PW)
                for oy in range(2):
                    pool.memset(by_oy[:, oy, :, R - R * oy, :], 0.0)
                    for ox in range(2):
                        last = pool.memset(tile[:, oy, :, ox, :, oy:oy + R, R - R * ox], 0.0)
                last.then_inc(s_zero, 1)

            with pool.Fori(0, n_batch // 2) as pair:
                for half in range(2):
                    b = pool.snap(2 * pair + half)
                    X, XN = BUF[half], BUF[1 - half]
                    for j in range(3):
                        clear_halo(j)
                    for s in range(2):
                        pool.memset(VTS[s].rearrange("p (u n) -> p u n", u=2)[:, :, P:P + 1], 1.0).then_inc(s_zero, 1)

                    def toeplitz(n):
                        t = n // 4
                        if n % 4 == 0:
                            pool.wait_ge(s_taps[t % 2], b * 96 + 16 * (t // 2 + 1))
                        if n >= 2:
                            wait_filled(pool, b, conv_item(n - 2))
                        dw = DW[t % 2].rearrange("p (h n) -> p h n", h=8)
                        for a in range(2):
                            hh = 2 * (n % 4) + a
                            o = TW[n % 2][:, a * CH:(a + 1) * CH].rearrange("p (k c q) -> p k c q", k=4, c=8)
                            tap = dw[:, hh, 0:64].rearrange("p (k q) -> p k q", k=4)
                            tap = tap.unsqueeze(2).broadcast_to([P, 4, 8, 16])
                            mix = dw[:, hh, 64:72].unsqueeze(1).unsqueeze(3).broadcast_to([P, 4, 8, 16])
                            last = pool.tensor_tensor(o, tap, mix, ALU.mult)
                        last.then_inc(s_tw, 1)

                    def add_to_x(n, i, buf, target):
                        pool.wait_ge(s_free[0], b * IT + 2 + count(i, 0))
                        pool.tensor_tensor(target, target, buf, ALU.add).then_inc(s_xp, 1)

                    for g in range(2):
                        for m in range(24):
                            toeplitz(24 * g + m)
                            if m == 9:
                                for k in range(3):
                                    pool.wait_ge(s_in[k], b * 512 + 32 * ((24 * g + 7 - k) // 3 + 1))
                                settle(pool)
                            if m >= 9 and m % 2:
                                chunk = chunk_of(RAW[0], (m - 9) // 2)
                                pool.tensor_scalar(chunk, chunk, 0.0, None, ALU.max).then_inc(s_qr, 1)
                        if g == 0:
                            wait_filled(pool, b, I_SUM1 + SUM_ITEMS[1] - 1)
                            settle(pool)
                            clear_halo(1)
                        for c in range(NCH):
                            add_to_x(8 * g + c, g * HALF_ITEMS + proj_item(c), planes(ADD0[c % 2]), x_planes(X, 0, c))
                    wait_filled(pool, b, L0_ITEMS - 1)
                    settle(pool)
                    pool.memset(kvb[:, :, 2 * D:KVW], 1.0)
                    pool.memset(KVT, 0.0)
                    for s in range(2):
                        last = pool.memset(VN[s].rearrange("p (t n) -> p t n", t=8)[:, :, D:D1], 1.0)
                    last.then_inc(s_zero1, 1)
                    for hp in range(2):
                        with pool.Fori(0, 2) as hl:
                            hd = b * NH + 2 * hp + hl
                            for p in range(TP):
                                sg = SG[p % 3].rearrange("p (u s d) -> p u s d", u=2, s=4)
                                feat = sg[:, :, 1:4:2, :]
                                rc = RC[:, 4 * (p % 3):4 * (p % 3) + 4].rearrange("p (u s) -> p u s", u=2)
                                pool.wait_ge(s_rc, hd * TP + p + 1)
                                pool.tensor_tensor(feat, feat, rc.unsqueeze(3).broadcast_to([P, 2, 2, D]),
                                                   ALU.mult).then_inc(s_nrm, 1)

                            def spread_q(start, u8):
                                src = QS[:, bass.ds(start + u8 * D, 2 * D)].rearrange("p (n c) -> p n c", n=2)
                                dst = QBD[:, u8 * P:(u8 + 2) * P].rearrange("p (n h c) -> p n h c", n=2, h=2)
                                pool.tensor_tensor(dst, src.unsqueeze(2).broadcast_to([P, 2, 2, D]),
                                                   HALVES.unsqueeze(1).unsqueeze(3).broadcast_to([P, 2, 2, D]),
                                                   ALU.mult).then_inc(s_qbd, 2)

                            def eight(nb, row, start, first):
                                for u8 in range(8):
                                    if u8 % 2 == 0 and not (first and u8 < 4):
                                        if not first:
                                            pool.wait_ge(s_o, nb + (u8 - 6))
                                            settle(pool)
                                        spread_q(start, u8)
                                    pool.load(pool_regs, IDXR[:, bass.ds(row + 8 * u8, 7)])
                                    off = [pool.snap(r, min_val=0, max_val=LAST) for r in pool_regs]
                                    if not (first and u8 < 4):
                                        pool.wait_ge(s_s, nb + (u8 - 3))
                                        settle(pool)
                                    for j in POOL_KEYS:
                                        last = pool.tensor_copy(GK[u8 % 4][:, j * D:(j + 1) * D],
                                                                KVB[:, bass.ds(off[j // 2 + 4 * (j % 2)], D)])
                                    last.then_inc(s_gk, 1)

                            pool.wait_ge(s_tbe, hd * TP + 4)
                            settle(pool)
                            for u8 in range(0, 4, 2):
                                spread_q(0, u8)
                            pool.wait_ge(s_tbe, (hd + 1) * TP)
                            settle(pool)
                            pool.wait_ge(s_ir[0], (b * 2 + hp + 1) * 16)
                            pool.wait_ge(s_ir[1], (b * 2 + hp + 1) * 16)
                            settle(pool)
                            eight(pool.snap(hd * NBLK), pool.snap(hl * (8 * NBLK)), 0, True)
                            with pool.Fori(1, 8) as qq:
                                eight(pool.snap(hd * NBLK + 8 * qq), pool.snap(hl * (8 * NBLK) + 64 * qq),
                                      pool.snap(qq * (8 * D)), False)
                        for k in range(8):
                            i = 2 * k
                            add_to_x(16 + 8 * hp + k, L0_ITEMS + D_ITEMS * hp + i, ADD1[k % 2],
                                     X[:, i // 8, (i % 8) * CH:(i % 8 + 1) * CH])
                    wait_filled(pool, b, ITEMS - 1)
                    settle(pool)

        @block.tensor
        def _(pe):
            pe.wait_ge(s_w, 16 * 7)
            for h in range(NH):
                last = nc.tensor.matmul(PS[:, h // 2, (h % 2) * C:(h % 2 + 1) * C], lhsT=arena[0:D, 0:P],
                                        rhs=WO[0:D, h, :], start=True, stop=True)
            last.then_inc(s_wo, 1)
            for ot in range(KT):
                for h in range(NH):
                    last = nc.tensor.matmul(PS[:, 2 + ot, 0:1], lhsT=WO[0:D, h, ot * P:(ot + 1) * P],
                                            rhs=LB[0:D, :], start=(h == 0), stop=(h == NH - 1))
            last.then_inc(s_wo, 1)
            pe.wait_ge(s_bias, 2)

            def group_sum(bn, layer, k):
                pe.wait_ge(s_mv, bn * 4 + 2 * layer + 1 + k)
                nc.tensor.matmul(PS[:, 6, 8 * k:8 * k + (4, 2)[k]], lhsT=same8, rhs=(MV, SQ)[k],
                                 start=True, stop=True).then_inc(s_gm, 1)

            for k in range(2):
                group_sum(0, 0, k)
            with pe.Fori(0, n_batch // 2) as pair:
                for half in range(2):
                    b = pe.snap(2 * pair + half)
                    X, XN = BUF[half], BUF[1 - half]
                    def bank(i):
                        return PS[:, i % 4, :]

                    def claim(i):
                        pe.wait_ge(s_free[i % 2], b * IT + i // 2 + 1)

                    def hand(i, ins):
                        ins.then_inc(s_it[i % 2], 1)

                    for g in range(2):
                        base = g * HALF_ITEMS

                        def conv(pairs, then=lambda m: None):
                            for m in pairs:
                                n = 24 * g + m
                                i = conv_item(n)
                                claim(i)
                                pe.wait_ge(s_tw, b * PAIRS + n + 1)
                                pe.wait_ge(s_in[n % 3], b * 512 + 32 * (n // 3 + 1))
                                for a in range(2):
                                    src = IN[n % 3][:, a * PAD:(a + 1) * PAD].rearrange("p (r c) -> p r c", r=PW)
                                    for k in range(4):
                                        last = nc.tensor.matmul(
                                            bank(i)[:, a * 256:(a + 1) * 256],
                                            lhsT=TW[n % 2][:, a * CH + k * P:a * CH + (k + 1) * P],
                                            rhs=src[:, k // 2:k // 2 + R, k % 2:k % 2 + R],
                                            start=(k == 0), stop=(k == 3))
                                hand(i, last)
                                then(m)

                        def kv_sums(src, half):
                            n_items = SUM_ITEMS[src]
                            start = base + (I_SUM0, I_SUM1)[src]

                            def add_up(t):
                                i = start + t
                                pe.wait_ge(s_free[i % 2], b * IT + 2 + count(i, i % 2))
                                for u in range(2):
                                    last = nc.tensor.matmul(PS[:, 4 + src, 0:P + 1],
                                                            lhsT=KTS[t % 2][:, u * P:(u + 1) * P],
                                                            rhs=VTS[t % 2][:, u * (P + 1):(u + 1) * (P + 1)],
                                                            start=(t == 0 and u == 0),
                                                            stop=(t == n_items - 1 and u == 1))
                                if t == n_items - 1:
                                    last.then_inc(s_kv, 1)
                            for t in range(n_items):
                                i = start + t
                                claim(i)
                                for u in range(2):
                                    nc.tensor.transpose(bank(i)[:, u * P:(u + 1) * P], half(1, 2 * t + u), ident)
                                    last = nc.tensor.transpose(bank(i)[:, (2 + u) * P:(3 + u) * P],
                                                               half(2, 2 * t + u), ident)
                                hand(i, last)
                                if t >= 1:
                                    add_up(t - 1)
                            add_up(n_items - 1)

                        def attend(src, c):
                            q = chunk_of(RAW[0], c) if src == 0 else AGG[0][:, c * CH:(c + 1) * CH]
                            for i, w in ((base + att_item(src, c), WD[src]), (base + att_item(src, c) + 1, WN[src])):
                                claim(i)
                                hand(i, nc.tensor.matmul(bank(i), lhsT=w, rhs=q, start=True, stop=True))

                        def attend_raw(c):
                            pe.wait_ge(s_qr, b * 16 + 8 * g + c + 1)
                            attend(0, c)

                        def wait_stored(n):
                            for k in range(3):
                                pe.wait_ge(s_og[k], b * 512 + 32 * ((n - k) // 3 + 2))

                        for j in range(3):
                            for c in range(NCH):
                                i = base + I_QKV + 8 * j + c
                                if g == 0 and j == 0 and c % 2 == 0:
                                    pe.wait_ge(s_xna, b * 8 + c // 2 + 1)
                                    pe.wait_ge(s_xnd, b * 8 + c // 2 + 1)
                                claim(i)
                                for kt in range(KT):
                                    last = nc.tensor.matmul(bank(i),
                                                            lhsT=W0[:, kt, (2 * j + g) * P:(2 * j + g + 1) * P],
                                                            rhs=XN[:, kt, c * CH:(c + 1) * CH],
                                                            start=(kt == 0), stop=(kt == KT - 1))
                                hand(i, last)
                        wait_emptied(pe, b, base + I_QKV + 23)
                        kv_sums(0, raw_half)
                        conv(range(8))
                        pe.wait_ge(s_w2, b * 4 + 2 * g + 1)
                        conv(range(8, 24), lambda m: m >= 11 and m % 2 and attend_raw((m - 11) // 2))
                        attend_raw(NCH - 1)
                        wait_stored(24 * g + 23)
                        kv_sums(1, agg_half)
                        pe.wait_ge(s_w2, b * 4 + 2 * g + 2)
                        for c in range(NCH + 2):
                            if c < NCH:
                                attend(1, c)
                            if c >= 2:
                                i = base + att_item(1, c - 2) + 1
                                pe.wait_ge(s_free[1], b * IT + 2 + count(i, 1))
                                for ot in range(KT):
                                    i = base + proj_item(c - 2) + ot
                                    claim(i)
                                    nc.tensor.matmul(bank(i), lhsT=WP[:, g, ot * P:(ot + 1) * P],
                                                     rhs=chunk_of(RAW[0], c - 2), start=True, stop=False)
                                    hand(i, nc.tensor.matmul(bank(i), lhsT=WP[:, 2 + g, ot * P:(ot + 1) * P],
                                                             rhs=AGG[0][:, (c - 2) * CH:(c - 1) * CH],
                                                             start=False, stop=True))

                    for k in range(2):
                        group_sum(b, 1, k)
                    pe.wait_ge(s_xbm, b + 1)
                    for h in range(NH):
                        for kt in range(KT):
                            last = nc.tensor.matmul(PS[:, 5, h * NBLK:(h + 1) * NBLK], lhsT=W1[:, kt, h, 0:2 * D],
                                                    rhs=XBM[:, kt, :], start=(kt == 0), stop=(kt == KT - 1))
                    last.then_inc(s_qkb, 1)
                    pe.wait_ge(s_qkc, b + 1)
                    settle(pe)
                    for h in range(NH):
                        cols = slice(h * NBLK, (h + 1) * NBLK)
                        last = nc.tensor.matmul(PS[0:D, 7, cols], lhsT=QB[0:D, cols], rhs=KB[0:D, cols],
                                                start=True, stop=True)
                    last.then_inc(s_sc, 1)
                    pe.wait_ge(s_zero1, b + 1)
                    for hp in range(2):
                        wait_emptied(pe, b, L0_ITEMS + D_ITEMS * hp - 1)
                        settle(pe)
                        with pe.Fori(0, 2) as hl:
                            hd = b * NH + 2 * hp + hl

                            def turn(p):
                                pe.wait_ge(s_nrm, hd * TP + p + 1)
                                if p == 0:
                                    pe.wait_ge(s_idx, b + 1)
                                if p >= 2:
                                    pe.wait_ge(s_tbe, hd * TP + p - 1)
                                sg = SG[p % 3]
                                vn = VN[p // 4 % 2]
                                for u in range(2):
                                    k_ck = sg[:, (4 * u + 2) * D:(4 * u + 4) * D]
                                    nc.tensor.transpose(PS[:, 2 + p % 2, u * P:(u + 1) * P],
                                                        sg[:, 4 * u * D:(4 * u + 2) * D], ident)
                                    nc.tensor.transpose(PS[:, 2 + p % 2, (2 + u) * P:(3 + u) * P], k_ck, ident)
                                for u in range(2):
                                    t = 2 * (p % 4) + u
                                    last = nc.tensor.matmul(PS[:, 7, 0:D1], lhsT=sg[:, (4 * u + 2) * D:(4 * u + 4) * D],
                                                            rhs=vn[:, t * D1:(t + 1) * D1],
                                                            start=(p == 0 and u == 0), stop=(p == TP - 1 and u == 1))
                                last.then_inc(s_tb, 1)

                            for p in range(TP):
                                if p >= 2:
                                    pe.wait_ge(s_raw, hd * TP + p - 1)
                                for u in range(2):
                                    t = 2 * p + u
                                    for kt in range(KT):
                                        last = nc.tensor.matmul(
                                            PS[:, p % 2, u * 3 * D:(u + 1) * 3 * D], lhsT=XN[:, kt, t * P:(t + 1) * P],
                                            rhs=W1[:, kt, bass.ds(2 * hp + hl, 1), :].rearrange("p o n -> p (o n)"),
                                            start=(kt == 0), stop=(kt == KT - 1))
                                last.then_inc(s_qp, 1)
                                if p >= 2:
                                    turn(p - 2)
                            turn(TP - 2)
                            turn(TP - 1)
                            pe.wait_ge(s_tbe, (hd + 1) * TP)
                            for k in range(2):
                                pe.wait_ge(s_vd[k], (hd + 1) * 128)
                            pe.wait_ge(s_kvt, hd + 1)
                            def turn_probs(nb, u):
                                pe.wait_ge(s_p, nb + (u + 1))
                                pe.wait_ge(s_lin, nb + (u + 1))
                                u8 = u % 8
                                for j in range(3):
                                    last = nc.tensor.transpose(PS[:, 2 + u8 % 2, j * P:(j + 1) * P],
                                                               PR[u8 % 2][:, j * P:(j + 1) * P], ident)
                                last.then_inc(s_t, 1)

                            def apply(nb, u):
                                pe.wait_ge(s_pt, nb + (u + 1))
                                pe.wait_ge(s_gva, nb + (u + 1))
                                pe.wait_ge(s_gvd, nb + (u + 1))
                                u8 = u % 8
                                o = PS[:, 4 + u8 // 4, (u8 % 4) * D1:(u8 % 4 + 1) * D1]
                                nc.tensor.matmul(o, lhsT=QBD[:, u8 * P:(u8 + 1) * P], rhs=KVT,
                                                 start=True, stop=False)
                                for k in range(TOPK // 2):
                                    last = nc.tensor.matmul(o, lhsT=PT[u8 % 2][:, k * P:(k + 1) * P],
                                                            rhs=GV[u8 % 4][:, k * D1:(k + 1) * D1],
                                                            start=False, stop=(k == TOPK // 2 - 1))
                                if u8 % 2:
                                    last.then_inc(s_o, 2)

                            def turn_out(quad, s):
                                pe.wait_ge(s_on, hd * 16 + quad + 1)
                                pe.wait_ge(s_one, hd * 16 + quad + 1)
                                for k in range(2):
                                    last = nc.tensor.transpose(PS[:, 6, (2 * s + k) * P:(2 * s + k + 1) * P],
                                                               ON[s][:, k * P:(k + 1) * P], ident)
                                last.then_inc(s_ont, 1)

                            def step(nb, u8, first, quad):
                                if not (first and u8 < 2):
                                    turn_probs(nb, u8 - 2)
                                if u8 % 2 == 0:
                                    pe.wait_ge(s_qbd, nb + (u8 + 2))
                                pe.wait_ge(s_gk, nb + (u8 + 1))
                                pe.wait_ge(s_gka, nb + (u8 + 1))
                                nc.tensor.matmul(PS[:, u8 % 2, 0:TOPK * D], lhsT=QBD[:, u8 * P:(u8 + 1) * P],
                                                 rhs=GK[u8 % 4], start=True, stop=True).then_inc(s_s, 1)
                                if not (first and u8 < 3):
                                    apply(nb, u8 - 3)
                                if u8 % 4 == 0 and not first:
                                    turn_out(quad - 2, u8 // 4)

                            nb = pe.snap(hd * NBLK)
                            for u8 in range(8):
                                step(nb, u8, True, u8 // 4)
                            with pe.Fori(1, 8) as qq:
                                nb = pe.snap(hd * NBLK + 8 * qq)
                                for u8 in range(8):
                                    step(nb, u8, False, 2 * qq + u8 // 4)
                            nb = hd * NBLK + NBLK
                            turn_probs(nb, -2)
                            apply(nb, -3)
                            turn_probs(nb, -1)
                            turn_out(14, 0)
                            apply(nb, -2)
                            apply(nb, -1)
                            turn_out(15, 1)
                        pe.wait_ge(s_one, b * 64 + 32 * (hp + 1) + 1)
                        for ot in range(KT):
                            for c in range(NCH):
                                i = L0_ITEMS + D_ITEMS * hp + NCH * ot + c
                                claim(i)
                                for hh in range(2):
                                    last = nc.tensor.matmul(bank(i), lhsT=WO[:, 2 * hp + hh, ot * P:(ot + 1) * P],
                                                            rhs=OT[:, hh * L + c * CH:hh * L + (c + 1) * CH],
                                                            start=(hh == 0), stop=(hh == 1))
                                hand(i, last)
                                if hp == 1 and NCH * ot + c in (9, 11):
                                    group_sum(b + 1, 0, (9, 11).index(NCH * ot + c))

        def empty_half(eng, e, b, g, copy, relu, weights, attend, project):
            base = g * HALF_ITEMS

            def conv(pairs, op):
                for m in pairs:
                    n = 24 * g + m
                    i = conv_item(n)
                    if i % 2 == e:
                        wait_filled(eng, b, i)
                        eng.wait_ge(s_og[n % 3], b * 512 + 32 * (n // 3 + 1))
                        op(OUTG[n % 3], PS[:, i % 4, :]).then_inc(s_free[e], 1)
                    if m >= 11 and m % 2:
                        attend(0, (m - 11) // 2)

            def turned(t, i):
                if i % 2 == e:
                    wait_filled(eng, b, i)
                    relu(KTS[t % 2], PS[:, i % 4, 0:2 * P])
                    copy(VTS[t % 2].rearrange("p (u n) -> p u n", u=2)[:, :, 0:P],
                         PS[:, i % 4, 2 * P:4 * P].rearrange("p (u n) -> p u n", u=2)).then_inc(s_free[e], 1)

            eng.wait_ge(s_zero, b * 6 + 5 + g)
            for j in range(3):
                for c in range(NCH):
                    i = base + I_QKV + 8 * j + c
                    if i % 2 == e:
                        wait_filled(eng, b, i)
                        copy(chunk_of(RAW[j], c), planes(PS[:, i % 4, :])).then_inc(s_free[e], 1)
            for t in range(SUM_ITEMS[0]):
                turned(t, base + I_SUM0 + t)
            weights(0)
            conv(range(8), relu)
            conv(range(8, 24), copy)
            attend(0, NCH - 1)
            for t in range(SUM_ITEMS[1]):
                turned(t, base + I_SUM1 + t)
            weights(1)
            for c in range(NCH + 2):
                if c < NCH:
                    attend(1, c)
                if c >= 2:
                    project(c - 2)

        def x_chunk(X, i):
            return X[:, i // NCH, (i % NCH) * CH:(i % NCH + 1) * CH]

        def norm_chunk(X, XN, layer, kt, q):
            if layer == 0:
                return (XN[:, kt, :].rearrange("p (fy fx r c) -> p fy fx r c", fy=4, fx=4, r=R)[:, q],
                        natural(X[:, kt, :], q))
            cols = slice(q * L // 4, (q + 1) * L // 4)
            return XN[:, kt, cols], X[:, kt, cols]

        @block.scalar
        def _(act):
            def copy(o, i):
                return nc.scalar.activation(o, i, ACT.Copy)

            def relu(o, i):
                return nc.scalar.activation(o, i, ACT.Relu)

            act.wait_ge(s_wo, 1)
            for h in range(NH):
                last = copy(WO[D:P, h, :], PS[D:P, h // 2, (h % 2) * C:(h % 2 + 1) * C])
            last.then_inc(s_bias, 1)
            act.sem_inc(s_free[0], 2)
            act_k_regs = [act.alloc_register(f"k_offset{k}") for k in range(2)]
            act_regs = [act.alloc_register(f"v_offset{k}") for k in range(3)]

            def root(bn, layer):
                act.wait_ge(s_var, bn * 2 + layer + 1)
                nc.scalar.activation(STD, VAR, ACT.Sqrt).then_inc(s_std, 1)

            root(0, 0)
            with act.Fori(0, n_batch // 2) as pair:
                for half in range(2):
                    b = act.snap(2 * pair + half)
                    X, XN = BUF[half], BUF[1 - half]
                    def scale(layer):
                        act.wait_ge(s_rstd, b * 2 + layer + 1)
                        for q in range(4):
                            if layer == 0:
                                act.wait_ge(s_st[1][q], b * 16 + 16)
                            dst, src = norm_chunk(X, XN, layer, 1, q)
                            nc.scalar.activation(dst, src, ACT.Identity, bias=NBIAS[:, 1:2],
                                                 scale=RSTD[:, 1:2]).then_inc(s_xna, 1)

                    def chunk_for_pool(n, i, buf, bias):
                        wait_filled(act, b, i)
                        if n % 8 >= 2:
                            act.wait_ge(s_xp, b * XADDS + n - 1)
                        nc.scalar.activation(buf, PS[:, i % 4, :], ACT.Identity, bias=bias).then_inc(s_free[0], 1)

                    scale(0)
                    for g in range(2):
                        def denominators(src, c):
                            i = g * HALF_ITEMS + att_item(src, c)
                            wait_filled(act, b, i)
                            k = 8 * src + c - 2
                            if k >= 0:
                                used = g * HALF_ITEMS + att_item(k // 8, k % 8) + 1
                                act.wait_ge(s_free[1], b * IT + 2 + count(used, 1))
                            nc.scalar.activation(DN[c % 2], PS[:, i % 4, :], ACT.Copy,
                                                 bias=ATT_EPS).then_inc(s_free[0], 1)

                        def project(c):
                            chunk_for_pool(8 * g + c, g * HALF_ITEMS + proj_item(c), ADD0[c % 2], 0.0)

                        empty_half(act, 0, b, g, copy, relu, lambda src: None, denominators, project)

                    root(b, 1)
                    scale(1)
                    act.wait_ge(s_qkb, b + 1)
                    copy(QB[0:D, :], PS[0:D, 5, 0:4 * NBLK])
                    copy(KB[0:D, :], PS[D:P, 5, 0:4 * NBLK]).then_inc(s_qkc, 1)
                    act.wait_ge(s_zero1, b + 1)
                    for hp in range(2):
                        act.wait_ge(s_xp, b * XADDS + 16 + 8 * hp)
                        settle(act)
                        with act.Fori(0, 2) as hl:
                            hd = b * NH + 2 * hp + hl

                            def store_turned(p):
                                act.wait_ge(s_tb, hd * TP + p + 1)
                                copy(kvb[:, 4 * p:4 * p + 4, 0:D],
                                     PS[:, 2 + p % 2, 2 * P:4 * P].rearrange("p (m n) -> p m n", m=4))
                                nc.scalar.activation(QS[:, p * 2 * P:(p + 1) * 2 * P], PS[:, 2 + p % 2, 0:2 * P],
                                                     ACT.Copy, scale=QSC).then_inc(s_tbe, 1)

                            for p in range(TP):
                                act.wait_ge(s_qp, hd * TP + p + 1)
                                if p % 4 == 0 and p >= 8:
                                    act.wait_ge(s_vd[p // 4 % 2], hd * 128 + 64 * (p // 8))
                                sg = SG[p % 3].rearrange("p (u s d) -> p u s d", u=2, s=4)
                                ps = PS[:, p % 2, 0:6 * D].rearrange("p (u s d) -> p u s d", u=2, s=3)
                                vn = VN[p // 4 % 2].rearrange("p (t n) -> p t n", t=8)
                                copy(sg[:, :, 0:4:2, :], ps[:, :, 0:2, :])
                                copy(vn[:, 2 * (p % 4):2 * (p % 4) + 2, 0:D], ps[:, :, 2, :]).then_inc(s_raw, 1)
                                if p >= 3:
                                    store_turned(p - 3)
                                act.wait_ge(s_sub, hd * TP + p + 1)
                                feat = sg[:, :, 1:4:2, :]
                                nc.scalar.activation(feat, feat, ACT.Exp).then_inc(s_exp, 1)
                            for p in range(TP - 3, TP):
                                store_turned(p)

                            def exp(nb, u):
                                act.wait_ge(s_nm, nb + (u + 1))
                                u8 = u % 8
                                nc.scalar.activation(PR[u8 % 2][0:D, :], PS[0:D, u8 % 2, 0:TOPK * D], ACT.Exp,
                                                     bias=NM[0:D, u8 % 2:u8 % 2 + 1]).then_inc(s_p, 1)

                            def store_probs(nb, u):
                                act.wait_ge(s_t, nb + (u + 1))
                                u8 = u % 8
                                copy(PT[u8 % 2], PS[:, 2 + u8 % 2, 0:TOPK * D]).then_inc(s_pt, 1)

                            def gather_v(row, u):
                                act.load(act_regs, IDXR[:, bass.ds(row + (8 * u + 4), 3)])
                                u8 = u % 8
                                for k in range(3):
                                    off = act.snap(act_regs[k], min_val=0, max_val=LAST)
                                    last = copy(GV[u8 % 4][D:P, k * D1:(k + 1) * D1], KVB[D:P, D:][:, bass.ds(off, D1)])
                                last.then_inc(s_gva, 1)

                            def gather_k(row, u8):
                                act.load(act_k_regs, IDXR[:, bass.ds(row + (8 * u8 + 4), 2)])
                                for k in range(2):
                                    off = act.snap(act_k_regs[k], min_val=0, max_val=LAST)
                                    last = copy(GK[u8 % 4][:, (2 * k + 1) * D:(2 * k + 2) * D], KVB[:, bass.ds(off, D)])
                                last.then_inc(s_gka, 1)

                            act.wait_ge(s_tbe, (hd + 1) * TP)
                            for k in range(2):
                                act.wait_ge(s_ir[k], (b * 2 + hp + 1) * 16)
                            settle(act)
                            nb, row = act.snap(hd * NBLK), act.snap(hl * (8 * NBLK))
                            for u8 in range(8):
                                gather_k(row, u8)
                                if u8 >= 2:
                                    exp(nb, u8 - 2)
                                    gather_v(row, u8 - 2)
                                if u8 >= 3:
                                    store_probs(nb, u8 - 3)
                            with act.Fori(1, 8) as qq:
                                nb, row = act.snap(hd * NBLK + 8 * qq), act.snap(hl * (8 * NBLK) + 64 * qq)
                                for u8 in range(8):
                                    gather_k(row, u8)
                                    exp(nb, u8 - 2)
                                    gather_v(row, u8 - 2)
                                    store_probs(nb, u8 - 3)
                            nb, row = act.snap(hd * NBLK + NBLK), act.snap((hl + 1) * (8 * NBLK))
                            for u in (-2, -1):
                                exp(nb, u)
                                gather_v(row, u)
                                store_probs(nb, u - 1)
                            store_probs(nb, -1)
                        for k in range(8):
                            chunk_for_pool(16 + 8 * hp + k, L0_ITEMS + D_ITEMS * hp + 2 * k, ADD1[k % 2],
                                           BIAS[:, k // 4:k // 4 + 1] if hp else 0.0)
                            if hp == 1 and k == 6:
                                root(b + 1, 0)

        @block.vector
        def _(dve):
            def copy(o, i):
                return nc.vector.tensor_copy(o, i)

            def relu(o, i):
                return nc.vector.tensor_scalar(o, i, 0.0, None, ALU.max)

            dve.wait_ge(s_wo, 2)
            nc.vector.tensor_copy(BIAS, PS[:, 2:4, 0]).then_inc(s_bias, 1)
            dve.sem_inc(s_free[1], 2)
            dve.sem_inc(s_one, 1)
            dve_regs = [dve.alloc_register(f"v_offset{k}") for k in range(3)]
            MOMENTS = 6
            DVE_N = 2 * MOMENTS + 4 + 4 * NCH + 3
            mv = MV.rearrange("p (k s) -> p k s", k=KT)
            gm = GM.rearrange("p (k s) -> p k s", k=KT)

            def chunk_stats(buf, n):
                return nc.vector.bn_stats(STATS[:, n // 8, n % 8, :], buf[:, n // 8, n % 8 * CH:(n % 8 + 1) * CH])

            def channel_moments(order, last):
                order.after(last)
                settle(dve)
                nc.vector.bn_aggr(mv[:, 0, :], STATS[:, 0])
                nc.vector.bn_aggr(mv[:, 1, :], STATS[:, 1]).then_inc(s_mv, 1)

            def deviations(order, bn, layer):
                dve.wait_ge(s_gm, bn * 4 + 2 * layer + 1)
                order.after(nc.vector.tensor_scalar(GM, PS[:, 6, 0:2 * KT], 1.0 / 8, None, ALU.mult))
                order.after(nc.vector.tensor_tensor(DEV, mv[:, :, 0], gm[:, :, 0], ALU.subtract))
                nc.vector.tensor_tensor(SQ, DEV, DEV, ALU.mult).then_inc(s_mv, 1)

            def variances(order, bn, layer):
                dve.wait_ge(s_gm, bn * 4 + 2 * layer + 2)
                order.after(nc.vector.scalar_tensor_tensor(out=VAR, in0=PS[:, 6, 8:8 + KT], scalar=1.0 / 8,
                                                           in1=gm[:, :, 1], op0=ALU.mult, op1=ALU.add))
                nc.vector.tensor_scalar(VAR, VAR, GN_EPS, None, ALU.add).then_inc(s_var, 1)

            def roots_inverse(order, bn, layer):
                dve.wait_ge(s_std, bn * 2 + layer + 1)
                order.after(nc.vector.reciprocal(RSTD, STD))
                order.after(nc.vector.tensor_tensor(NBIAS, gm[:, :, 0], RSTD, ALU.mult))
                nc.vector.tensor_scalar(NBIAS, NBIAS, -1.0, None, ALU.mult).then_inc(s_rstd, 1)

            first = Order(dve, s_dve, 0, MOMENTS)
            dve.wait_ge(s_ld, 32)
            for n in range(16):
                last = chunk_stats(BUF[0], n)
            channel_moments(first, last)
            deviations(first, 0, 0)
            variances(first, 0, 0)
            roots_inverse(first, 0, 0)
            first.close()
            with dve.Fori(0, n_batch // 2) as pair:
                for half in range(2):
                    b = dve.snap(2 * pair + half)
                    X, XN = BUF[half], BUF[1 - half]
                    order = Order(dve, s_dve, b * DVE_N + MOMENTS, DVE_N)

                    def scale(layer):
                        for q in range(4):
                            if layer == 0:
                                dve.wait_ge(s_st[0][q], b * 16 + 16)
                            dst, src = norm_chunk(X, XN, layer, 0, q)
                            nc.vector.tensor_scalar(dst, src, GM[:, 0:1], RSTD[:, 0:1], ALU.subtract,
                                                    ALU.mult).then_inc(s_xnd, 1)

                    scale(0)
                    def plane_stats(kt, c):
                        if kt:
                            dve.wait_ge(s_free[1], b * IT + 2 + count(HALF_ITEMS + proj_item(c) + 1, 1))
                        else:
                            dve.wait_ge(s_xp, b * XADDS + 8 + c + 1)
                        return nc.vector.bn_stats(STATS[:, kt, c, :], x_planes(X, kt, c))

                    for g in range(2):
                        def kv_weights(src):
                            dve.wait_ge(s_kv, b * 4 + 2 * g + src + 1)
                            order.after(nc.vector.tensor_copy(KSUM[:, src:src + 1], PS[:, 4 + src, P:P + 1]))
                            nc.vector.tensor_tensor(WN[src], PS[:, 4 + src, 0:P], same8, ALU.mult)
                            nc.vector.tensor_scalar(WD[src], same8, KSUM[:, src:src + 1], None,
                                                    ALU.mult).then_inc(s_w2, 1)

                        def divide(src, c):
                            i = g * HALF_ITEMS + att_item(src, c)
                            dve.wait_ge(s_free[0], b * IT + 2 + count(i, 0))
                            order.after(nc.vector.reciprocal(DN[c % 2], DN[c % 2]))
                            wait_filled(dve, b, i + 1)
                            ps = PS[:, (i + 1) % 4, :]
                            if src == 0:
                                nc.vector.tensor_tensor(chunk_of(RAW[0], c), planes(ps), planes(DN[c % 2]),
                                                        ALU.mult).then_inc(s_free[1], 1)
                            else:
                                nc.vector.tensor_tensor(AGG[0][:, c * CH:(c + 1) * CH], ps, DN[c % 2],
                                                        ALU.mult).then_inc(s_free[1], 1)

                        def project(c):
                            i = g * HALF_ITEMS + proj_item(c) + 1
                            wait_filled(dve, b, i)
                            nc.vector.tensor_tensor(x_planes(X, 1, c), planes(PS[:, i % 4, :]), x_planes(X, 1, c),
                                                    ALU.add).then_inc(s_free[1], 1)
                            if g == 1 and c >= 1:
                                plane_stats(1, c - 1)
                            if g == 1 and c >= 3:
                                plane_stats(0, c - 3)

                        empty_half(dve, 1, b, g, copy, relu, kv_weights, divide, project)

                    plane_stats(1, NCH - 1)
                    for c in range(NCH - 3, NCH):
                        last = plane_stats(0, c)
                    channel_moments(order, last)
                    deviations(order, b, 1)
                    variances(order, b, 1)
                    roots_inverse(order, b, 1)
                    scale(1)
                    dve.wait_ge(s_xnd, b * 8 + 8)
                    nc.vector.tensor_reduce(XBM[:, 0, :], XN[:, 0, :].rearrange("p (m t) -> p m t", m=NBLK), AX.X,
                                            ALU.add)
                    dve.wait_ge(s_xna, b * 8 + 8)
                    nc.vector.tensor_reduce(XBM[:, 1, :], XN[:, 1, :].rearrange("p (m t) -> p m t", m=NBLK), AX.X,
                                            ALU.add).then_inc(s_xbm, 1)
                    dve.wait_ge(s_sc, b + 1)
                    order.after(copy(SC[0:D, :], PS[0:D, 7, 0:4 * NBLK]))
                    settle(dve)
                    for h in range(NH):
                        last = nc.vector.max(MX8[0:D, 8 * h:8 * h + 8], SC[0:D, h * NBLK:(h + 1) * NBLK])
                    order.after(last)
                    settle(dve)
                    for h in range(NH):
                        last = nc.vector.max_index(IU[:, 8 * h:8 * h + 8], MX8[0:D, 8 * h:8 * h + 8],
                                                   SC[0:D, h * NBLK:(h + 1) * NBLK])
                    order.after(last)
                    idx, iu = IDX[:].rearrange("p (h k) -> p h k", h=NH), IU.rearrange("p (h k) -> p h k", h=NH)
                    nc.vector.tensor_scalar(idx[:, :, 0:4], iu[:, :, 0:4], float(KVW), None, ALU.mult)
                    nc.vector.tensor_scalar(idx[:, :, 4:8], iu[:, :, 3:7], float(KVW), None,
                                            ALU.mult).then_inc(s_idx, 1)
                    for hp in range(2):
                        with dve.Fori(0, 2) as hl:
                            hd = b * NH + 2 * hp + hl
                            torder = Order(dve, s_dveb, hd * 2 * TP, 2 * TP)

                            def sums(p):
                                dve.wait_ge(s_exp, hd * TP + p + 1)
                                feat = SG[p % 3].rearrange("p (u s d) -> p u s d", u=2, s=4)[:, :, 1:4:2, :]
                                part = slice(4 * (p % 3), 4 * (p % 3) + 4)
                                su = SU[:, part].rearrange("p (u s) -> p u s", u=2)
                                torder.after(nc.vector.tensor_reduce(su, feat, AX.X, ALU.add))
                                nc.vector.reciprocal(RC[:, part], SU[:, part]).then_inc(s_rc, 1)

                            for p in range(TP):
                                if p >= 1:
                                    sums(p - 1)
                                dve.wait_ge(s_raw, hd * TP + p + 1)
                                sg = SG[p % 3].rearrange("p (u s d) -> p u s d", u=2, s=4)
                                qk, feat = sg[:, :, 0:4:2, :], sg[:, :, 1:4:2, :]
                                mx = MX[:, 4 * (p % 3):4 * (p % 3) + 4].rearrange("p (u s) -> p u s", u=2)
                                torder.after(nc.vector.tensor_reduce(mx, qk, AX.X, ALU.max))
                                nc.vector.tensor_tensor(feat, qk, mx.unsqueeze(3).broadcast_to([P, 2, 2, D]),
                                                        ALU.subtract).then_inc(s_sub, 1)
                            sums(TP - 1)
                            torder.close()
                            dve.wait_ge(s_tb, (hd + 1) * TP)
                            nc.vector.tensor_scalar(KVT[D:P, :], PS[D:P, 7, 0:D1], -1.0, None,
                                                    ALU.mult).then_inc(s_kvt, 1)

                            def maxima(nb, u8):
                                dve.wait_ge(s_s, nb + (u8 + 1))
                                nc.vector.tensor_reduce(NM[0:D, u8 % 2:u8 % 2 + 1], PS[0:D, u8 % 2, 0:TOPK * D], AX.X,
                                                        ALU.max, negate=True).then_inc(s_nm, 1)
                                copy(PR[u8 % 2][D:P, :], PS[D:P, u8 % 2, 0:TOPK * D]).then_inc(s_lin, 1)

                            def normalise_out(quad, s):
                                o = PS[:, 4 + s, 0:4 * D1].rearrange("p (n c) -> p n c", n=4)
                                chain = hd * 32 + 2 * quad
                                dve.wait_ge(s_o, hd * NBLK + 4 * quad + 4)
                                nc.vector.tensor_scalar(DNQ.unsqueeze(2), o[:, :, D:D1], EPSV, None,
                                                        ALU.add).then_inc(s_dvec, 1)
                                dve.wait_ge(s_dvec, chain + 1)
                                nc.vector.reciprocal(RNQ, DNQ).then_inc(s_dvec, 1)
                                dve.wait_ge(s_dvec, chain + 2)
                                on = ON[s].rearrange("p (k c) -> p k c", k=2)
                                for u in range(2):
                                    for lin in range(2):
                                        rows = slice(D * lin, D * (lin + 1))
                                        last = nc.vector.tensor_tensor(
                                            on[D * u:D * (u + 1), :, D * lin:D * (lin + 1)], o[rows, u:4:2, 0:D],
                                            RNQ[rows, u:4:2].unsqueeze(2).broadcast_to([D, 2, D]), ALU.mult)
                                last.then_inc(s_on, 1)

                            def store_out(quad, s):
                                dve.wait_ge(s_ont, hd * 16 + quad + 1)
                                copy(OT[:, bass.ds(hl * L + quad * 4 * D, 4 * D)],
                                     PS[:, 6, 2 * s * P:(2 * s + 2) * P]).then_inc(s_one, 1)

                            def gather_v(row, u8):
                                dve.load(dve_regs, IDXR[:, bass.ds(row + 8 * u8, 3)])
                                for k in range(3):
                                    off = dve.snap(dve_regs[k], min_val=0, max_val=LAST)
                                    last = copy(GV[u8 % 4][0:D, k * D1:(k + 1) * D1], KVB[0:D, D:][:, bass.ds(off, D1)])
                                last.then_inc(s_gvd, 1)

                            def step(nb, row, u8, first, quad):
                                maxima(nb, u8)
                                gather_v(row, u8)
                                if u8 % 4 == 1 and not (first and u8 <= 5):
                                    store_out(quad - 2, u8 // 4)
                                if u8 % 4 == 3 and not (first and u8 == 3):
                                    normalise_out(quad - 1, (u8 // 4 + 1) % 2)

                            nb, row = dve.snap(hd * NBLK), dve.snap(hl * (8 * NBLK))
                            for u8 in range(8):
                                step(nb, row, u8, True, u8 // 4)
                            with dve.Fori(1, 8) as qq:
                                nb, row = dve.snap(hd * NBLK + 8 * qq), dve.snap(hl * (8 * NBLK) + 64 * qq)
                                for u8 in range(8):
                                    step(nb, row, u8, False, 2 * qq + u8 // 4)
                            store_out(14, 0)
                            normalise_out(15, 1)
                            store_out(15, 1)
                        for k in range(8):
                            i = 2 * k + 1
                            wait_filled(dve, b, L0_ITEMS + D_ITEMS * hp + i)
                            xc = x_chunk(X, i)
                            if hp == 0:
                                ins = nc.vector.tensor_tensor(xc, PS[:, i % 4, :], xc, ALU.add)
                            else:
                                ins = nc.vector.scalar_tensor_tensor(out=xc, in0=PS[:, i % 4, :],
                                                                     scalar=BIAS[:, i // NCH:i // NCH + 1], in1=xc,
                                                                     op0=ALU.add, op1=ALU.add)
                            ins.then_inc(s_free[1], 1)
                            if hp == 1 and k < 4:
                                if k == 0:
                                    dve.wait_ge(s_ld, (b + 2) * 32)
                                for n in range(4 * k, 4 * k + 4):
                                    last = chunk_stats(XN, n)
                            if hp == 1 and k == 3:
                                channel_moments(order, last)
                            elif hp == 1 and k == 4:
                                deviations(order, b + 1, 0)
                            elif hp == 1 and k == 5:
                                variances(order, b + 1, 0)
                            elif hp == 1 and k == 6:
                                roots_inverse(order, b + 1, 0)
                    order.close()


def kernel(**inputs):
    import numpy as np
    import concourse.bacc as bacc
    from concourse.bass_utils import run_bass_kernel_spmd as run

    x = np.ascontiguousarray(inputs["x"])
    n_batch = x.shape[0]
    a = {"x": x.reshape(n_batch, KT, P, L)}
    perm = (24 * np.arange(32)[None, :, None] + 8 * np.arange(3)[:, None, None] + np.arange(8)).reshape(-1)
    w = np.asarray(inputs["L0_conv_w_qkv"])[perm, :, 0, 0]
    a["w0"] = w.T.reshape(KT, P, 3 * C).transpose(1, 0, 2)
    dw = np.asarray(inputs["L0_conv_w_dw"])[perm, 0]
    padded = np.pad(dw, ((0, 0), (3, 3), (3, 3)))
    plane = (np.arange(4) + 2) % 4
    t = 4 * np.arange(2)[None, :, None] + plane[:, None, None] - np.arange(4)[None, None, :] + 3
    tt = padded[:, t[:, :, :, None, None, None], t[None, None, None]]
    tt = tt.transpose(0, 1, 4, 2, 5, 3, 6).reshape(96, 8 * 16, 64)
    pw = np.asarray(inputs["L0_conv_w_pw"])[perm, :, 0, 0].reshape(96, 8, 8)
    pw = np.repeat(pw.transpose(0, 2, 1), 16, axis=1)
    a["taps"] = np.concatenate([tt, pw], axis=2).reshape(6, 2, 8, P, TAPS).transpose(0, 1, 3, 2, 4).reshape(
        6, 2, P, 8 * TAPS)
    a["wp"] = np.asarray(inputs["L0_conv_w_proj"])[:, :, 0, 0].T.reshape(4, P, C).transpose(1, 0, 2)
    w = np.asarray(inputs["L1_conv_qkv_w"]).reshape(3, NH, D, C)
    a["w1"] = w.transpose(3, 1, 0, 2).reshape(KT, P, NH, 3 * D).transpose(1, 0, 2, 3)
    a["wo"] = np.asarray(inputs["L1_conv_out_w"]).T.reshape(NH, D, C).transpose(1, 0, 2)
    a["lw"] = np.pad(np.asarray(inputs["L1_conv_proj_lw"]), ((0, 0), (D, 0)))
    a["lb"] = np.asarray(inputs["L1_conv_proj_lb"])[:, None]
    group = np.arange(P) // 8
    lower = np.arange(P)[:, None] >= D
    a["consts"] = np.concatenate([np.eye(P), group[:, None] == group[None, :], ~lower, lower, -LIN_EPS * lower,
                                  np.where(lower, 1.0, D ** -0.5)],
                                 axis=1).astype(np.float32)

    nc = bacc.Bacc("TRN2", target_bir_lowering=False, num_devices=1)
    arrays, args = {}, []
    for name, v in a.items():
        v = np.ascontiguousarray(v)
        arrays[f"in_{name}"] = v
        args.append(nc.dram_tensor(f"in_{name}", v.shape, mybir.dt.from_np(v.dtype), kind="ExternalInput").ap())
    out = nc.dram_tensor("out", (n_batch, KT, P, L), F32, kind="ExternalOutput").ap()
    build(nc, *args, out, n_batch)
    r = run(nc, [arrays], core_ids=[0])
    return r.results[0]["out"].reshape(n_batch, C, HH, WW)
```
